# Optimizing a Trainium2 kernel written in Bass

```python
import numpy as np
import jax
import jax.numpy as jnp

def _softmax(x, axis=-1):
    return jax.nn.softmax(x, axis=axis)

def _gelu(x):
    return jax.nn.gelu(x, approximate=True)

def _silu(x):
    return jax.nn.silu(x)

def _sigmoid(x):
    return jax.nn.sigmoid(x)

def _layernorm(x, axis=-1, eps=1e-05):
    m = jnp.mean(x, axis=axis, keepdims=True)
    v = jnp.var(x, axis=axis, keepdims=True)
    return (x - m) / jnp.sqrt(v + eps)

def _scatter_add(tgt, idx, src, axis=0):
    return tgt.at[idx].add(src)

def _segment_sum(src, seg, n):
    return jax.ops.segment_sum(src, seg, n)
kernel_name = 'mk_adj_resnorm_d4_adj_r2_bde596'

def setup_inputs(seed: int=0):
    np.random.seed(seed)
    _w = jnp.asarray

    def _rec_inputs():
        import jax
        import jax.numpy as jnp
        _gk = jax.random.key(seed)
        x = 7.22e-05 + 1 * jax.random.normal(jax.random.fold_in(_gk, 1), (16, 512, 128), jnp.float32)
        _w = (1.0 + jnp.arange(512, dtype=jnp.float32)) ** (-0.5)
        _w = _w / _w.mean()
        _pij = jnp.clip(0.0078125 * _w[:, None] * _w[None, :], 0.0, 1.0)
        _a = jax.random.uniform(jax.random.fold_in(_gk, 2), (16, 512, 512)) < _pij
        _a = jnp.logical_or(_a, jnp.swapaxes(_a, -1, -2))
        _a = jnp.logical_or(_a, jnp.eye(512, dtype=bool))
        _af = _a.astype(jnp.float32)
        adj = _af
        _nm = jnp.ones((16, 512), dtype=bool)
        nodemask = jnp.where(_nm, 1.0, 0.0).astype(jnp.float32)
        return (x, adj, nodemask)
    x, adj, nodemask = _rec_inputs()

    def _L0_gnn_setup():
        import jax, jax.numpy as jnp
        import numpy as np
        from jax import lax
        DIM = 128
        EPS = 1e-05

        def _bn(h, g, b, m, v):
            scale = g / jnp.sqrt(v + EPS)
            return h * scale[None, :, None] + (b - m * scale)[None, :, None]

        def _conv1d(h, w, pad):
            return lax.conv_general_dilated(h, w, window_strides=(1,), padding=[(pad, pad)], dimension_numbers=('NCH', 'OIH', 'NCH'))
        key = jax.random.key(seed)
        ks = jax.random.split(key, 16)
        bs, n, d = (16, 1024, DIM)
        s = 0.05
        return {'x': jax.random.normal(ks[0], (bs, n, d), jnp.float32), 'mask': jnp.ones((bs, n, n), jnp.float32), 'w_se': jax.random.normal(ks[1], (3, d), jnp.float32) * s, 'b_se': jnp.zeros((3,), jnp.float32), 'conv1_w': jax.random.normal(ks[2], (d, d, 1), jnp.float32) * s, 'bn1_g': jnp.ones((d,), jnp.float32), 'bn1_b': jnp.zeros((d,), jnp.float32), 'bn1_m': jnp.zeros((d,), jnp.float32), 'bn1_v': jnp.ones((d,), jnp.float32), 'conv2_w': jax.random.normal(ks[3], (d, d, 17), jnp.float32) * s, 'bn2_g': jnp.ones((d,), jnp.float32), 'bn2_b': jnp.zeros((d,), jnp.float32), 'bn2_m': jnp.zeros((d,), jnp.float32), 'bn2_v': jnp.ones((d,), jnp.float32), 'w_msg': jax.random.normal(ks[4], (d, d), jnp.float32) * s, 'b_msg': jnp.zeros((d,), jnp.float32), 'w_ih': jax.random.normal(ks[5], (3 * d, 2 * d), jnp.float32) * s, 'b_ih': jnp.zeros((3 * d,), jnp.float32), 'w_hh': jax.random.normal(ks[6], (3 * d, d), jnp.float32) * s, 'b_hh': jnp.zeros((3 * d,), jnp.float32)}
    _L0_gnn_all = _L0_gnn_setup()
    _L0_gnn_in = {k: v for k, v in _L0_gnn_all.items() if k in ('w_se', 'b_se', 'conv1_w', 'bn1_g', 'bn1_b', 'bn1_m', 'bn1_v', 'conv2_w', 'bn2_g', 'bn2_b', 'bn2_m', 'bn2_v', 'w_msg', 'b_msg', 'w_ih', 'b_ih', 'w_hh', 'b_hh')}
    del _L0_gnn_all

    def _L1_gnn_setup():
        import jax, jax.numpy as jnp
        import numpy as np
        NEG_SLOPE = 0.01

        def leaky_relu(x):
            return jnp.where(x >= 0, x, NEG_SLOPE * x)
        key = jax.random.key(seed)
        ks = jax.random.split(key, 6)
        B, N, in_dim, out_dim = (8, 1024, 128, 128)
        node_feats = jax.random.normal(ks[0], (B, N, in_dim), dtype=jnp.float32)
        adj_matrix = jax.random.uniform(ks[1], (B, N, N), dtype=jnp.float32)
        s_in = (2.0 / in_dim) ** 0.5
        W_lin = jax.random.normal(ks[2], (in_dim, out_dim), dtype=jnp.float32) * s_in
        b_lin = jnp.zeros((out_dim,), dtype=jnp.float32)
        W_q = jax.random.normal(ks[3], (in_dim, out_dim), dtype=jnp.float32) * s_in
        W_k = jax.random.normal(ks[4], (in_dim, out_dim), dtype=jnp.float32) * s_in
        return {'node_feats': node_feats, 'adj_matrix': adj_matrix, 'W_lin': W_lin, 'b_lin': b_lin, 'W_q': W_q, 'W_k': W_k}
    _L1_gnn_all = _L1_gnn_setup()
    _L1_gnn_in = {k: v for k, v in _L1_gnn_all.items() if k in ('W_lin', 'b_lin', 'W_q', 'W_k')}
    del _L1_gnn_all

    def _L2_gnn_setup():
        import jax, jax.numpy as jnp
        import numpy as np
        C = 1.0
        SQRT_C = jnp.float32(np.sqrt(C))
        MIN_NORM = 1e-15
        BALL_EPS = 0.004

        def _norm(x):
            return jnp.clip(jnp.linalg.norm(x, axis=-1, keepdims=True), MIN_NORM, None)

        def _artanh(x):
            return jnp.arctanh(jnp.clip(x, -1 + 1e-07, 1 - 1e-07))

        def logmap0(x):
            n = _norm(x)
            return _artanh(SQRT_C * n) * x / (SQRT_C * n)

        def expmap0(u):
            n = _norm(u)
            return jnp.tanh(SQRT_C * n) * u / (SQRT_C * n)

        def project(x):
            n = _norm(x)
            maxnorm = (1.0 - BALL_EPS) / SQRT_C
            return jnp.where(n > maxnorm, x * (maxnorm / n), x)
        key = jax.random.key(seed)
        k1, k2 = jax.random.split(key)
        B, N, D = (2, 4096, 128)
        x = project(expmap0(0.1 * jax.random.normal(k1, (B, N, D), dtype=jnp.float32)))
        adj = jax.random.uniform(k2, (B, N, N), dtype=jnp.float32) / N
        return {'x': x, 'adj': adj}
    _L2_gnn_all = _L2_gnn_setup()
    _L2_gnn_in = {k: v for k, v in _L2_gnn_all.items() if k in ()}
    del _L2_gnn_all

    def _L3_gnn_setup():
        import jax, jax.numpy as jnp
        import numpy as np
        EPS = 1e-08
        key = jax.random.key(seed)
        kH, kA, kW = jax.random.split(key, 3)
        B, N, IN, OUT = (32, 256, 128, 128)
        H = jax.random.normal(kH, (B, N, IN), dtype=jnp.float32)
        A = jax.random.uniform(kA, (B, N, N), dtype=jnp.float32)
        mask = jnp.ones((B, N), dtype=jnp.float32)
        W = jax.random.normal(kW, (OUT, IN), dtype=jnp.float32) * (1.0 / np.sqrt(IN))
        b = jnp.zeros((OUT,), dtype=jnp.float32)
        return {'H': H, 'A': A, 'mask': mask, 'W': W, 'b': b}
    _L3_gnn_all = _L3_gnn_setup()
    _L3_gnn_in = {k: v for k, v in _L3_gnn_all.items() if k in ('W', 'b')}
    del _L3_gnn_all
    return {'x': x, 'adj': adj, 'nodemask': nodemask, 'L0_gnn_w_se': _L0_gnn_in['w_se'], 'L0_gnn_b_se': _L0_gnn_in['b_se'], 'L0_gnn_conv1_w': _L0_gnn_in['conv1_w'], 'L0_gnn_bn1_g': _L0_gnn_in['bn1_g'], 'L0_gnn_bn1_b': _L0_gnn_in['bn1_b'], 'L0_gnn_bn1_m': _L0_gnn_in['bn1_m'], 'L0_gnn_bn1_v': _L0_gnn_in['bn1_v'], 'L0_gnn_conv2_w': _L0_gnn_in['conv2_w'], 'L0_gnn_bn2_g': _L0_gnn_in['bn2_g'], 'L0_gnn_bn2_b': _L0_gnn_in['bn2_b'], 'L0_gnn_bn2_m': _L0_gnn_in['bn2_m'], 'L0_gnn_bn2_v': _L0_gnn_in['bn2_v'], 'L0_gnn_w_msg': _L0_gnn_in['w_msg'], 'L0_gnn_b_msg': _L0_gnn_in['b_msg'], 'L0_gnn_w_ih': _L0_gnn_in['w_ih'], 'L0_gnn_b_ih': _L0_gnn_in['b_ih'], 'L0_gnn_w_hh': _L0_gnn_in['w_hh'], 'L0_gnn_b_hh': _L0_gnn_in['b_hh'], 'L1_gnn_W_lin': _L1_gnn_in['W_lin'], 'L1_gnn_b_lin': _L1_gnn_in['b_lin'], 'L1_gnn_W_q': _L1_gnn_in['W_q'], 'L1_gnn_W_k': _L1_gnn_in['W_k'], 'L3_gnn_W': _L3_gnn_in['W'], 'L3_gnn_b': _L3_gnn_in['b']}

def reference(x, adj, nodemask, L0_gnn_w_se, L0_gnn_b_se, L0_gnn_conv1_w, L0_gnn_bn1_g, L0_gnn_bn1_b, L0_gnn_bn1_m, L0_gnn_bn1_v, L0_gnn_conv2_w, L0_gnn_bn2_g, L0_gnn_bn2_b, L0_gnn_bn2_m, L0_gnn_bn2_v, L0_gnn_w_msg, L0_gnn_b_msg, L0_gnn_w_ih, L0_gnn_b_ih, L0_gnn_w_hh, L0_gnn_b_hh, L1_gnn_W_lin, L1_gnn_b_lin, L1_gnn_W_q, L1_gnn_W_k, L3_gnn_W, L3_gnn_b):
    import jax
    import jax.numpy as jnp

    def _L0_gnn_ref(x, mask, w_se, b_se, conv1_w, bn1_g, bn1_b, bn1_m, bn1_v, conv2_w, bn2_g, bn2_b, bn2_m, bn2_v, w_msg, b_msg, w_ih, b_ih, w_hh, b_hh):
        import jax, jax.numpy as jnp
        import numpy as np
        from jax import lax
        DIM = 128
        EPS = 1e-05

        def _bn(h, g, b, m, v):
            scale = g / jnp.sqrt(v + EPS)
            return h * scale[None, :, None] + (b - m * scale)[None, :, None]

        def _conv1d(h, w, pad):
            return lax.conv_general_dilated(h, w, window_strides=(1,), padding=[(pad, pad)], dimension_numbers=('NCH', 'OIH', 'NCH'))
        d = x.shape[-1]
        xc = jnp.transpose(x, (0, 2, 1))
        h = _bn(_conv1d(xc, conv1_w, 0), bn1_g, bn1_b, bn1_m, bn1_v)
        h = jax.nn.relu(h)
        h = _bn(_conv1d(h, conv2_w, 8), bn2_g, bn2_b, bn2_m, bn2_v)
        x_conv = jnp.transpose(jax.nn.relu(h + xc), (0, 2, 1))
        s = x @ w_se.T + b_se
        sq = jnp.sum(s * s, axis=-1)
        dist = sq[:, :, None] + sq[:, None, :] - 2.0 * jnp.einsum('bnd,bmd->bnm', s, s)
        A = jnp.exp(-dist) * mask
        msg = jax.nn.relu(x @ w_msg.T + b_msg)
        x_nmp = jnp.einsum('bnm,bmd->bnd', A, msg)
        x_in = jnp.concatenate([x_conv, x_nmp], axis=-1)
        gi = x_in @ w_ih.T + b_ih
        gh = x @ w_hh.T + b_hh
        gi_r, gi_z, gi_n = (gi[..., :d], gi[..., d:2 * d], gi[..., 2 * d:])
        gh_r, gh_z, gh_n = (gh[..., :d], gh[..., d:2 * d], gh[..., 2 * d:])
        r = jax.nn.sigmoid(gi_r + gh_r)
        z = jax.nn.sigmoid(gi_z + gh_z)
        nn_ = jnp.tanh(gi_n + r * gh_n)
        return (1.0 - z) * nn_ + z * x

    def _L1_gnn_ref(node_feats, adj_matrix, W_lin, b_lin, W_q, W_k):
        import jax, jax.numpy as jnp
        import numpy as np
        NEG_SLOPE = 0.01

        def leaky_relu(x):
            return jnp.where(x >= 0, x, NEG_SLOPE * x)
        out_dim = W_lin.shape[1]
        scale = out_dim ** (-0.5)
        X = leaky_relu(node_feats @ W_lin + b_lin)
        q = leaky_relu(node_feats @ W_q)
        k = leaky_relu(node_feats @ W_k)
        att = jax.nn.sigmoid(jnp.einsum('bxh,byh->bxy', q, k) * scale)
        A = adj_matrix * att
        d = jnp.sum(A, axis=-1)
        d_inv_sqrt = d ** (-0.5)
        d_inv_sqrt = jnp.where(jnp.isinf(d_inv_sqrt), 0.0, d_inv_sqrt)
        A_norm = d_inv_sqrt[:, :, None] * A * d_inv_sqrt[:, None, :]
        return jnp.einsum('bxy,byh->bxh', A_norm, X)

    def _L2_gnn_ref(x, adj):
        import jax, jax.numpy as jnp
        import numpy as np
        C = 1.0
        SQRT_C = jnp.float32(np.sqrt(C))
        MIN_NORM = 1e-15
        BALL_EPS = 0.004

        def _norm(x):
            return jnp.clip(jnp.linalg.norm(x, axis=-1, keepdims=True), MIN_NORM, None)

        def _artanh(x):
            return jnp.arctanh(jnp.clip(x, -1 + 1e-07, 1 - 1e-07))

        def logmap0(x):
            n = _norm(x)
            return _artanh(SQRT_C * n) * x / (SQRT_C * n)

        def expmap0(u):
            n = _norm(u)
            return jnp.tanh(SQRT_C * n) * u / (SQRT_C * n)

        def project(x):
            n = _norm(x)
            maxnorm = (1.0 - BALL_EPS) / SQRT_C
            return jnp.where(n > maxnorm, x * (maxnorm / n), x)
        x_tangent = logmap0(x)
        support_t = jnp.einsum('bij,bjd->bid', adj, x_tangent)
        return project(expmap0(support_t))

    def _L3_gnn_ref(H, A, mask, W, b):
        import jax, jax.numpy as jnp
        import numpy as np
        EPS = 1e-08
        N = A.shape[-1]
        A_hat = A + jnp.eye(N, dtype=A.dtype)
        deg = A_hat.sum(axis=-1)
        dis = (deg + EPS) ** (-0.5)
        A_norm = dis[:, :, None] * A_hat * dis[:, None, :]
        H_lin = jnp.einsum('bni,oi->bno', H, W) + b
        out = jnp.einsum('bnm,bmo->bno', A_norm, H_lin)
        out = out * mask[:, :, None]
        return jax.nn.relu(out)
    x = _layernorm(x + _L0_gnn_ref(x, adj, L0_gnn_w_se, L0_gnn_b_se, L0_gnn_conv1_w, L0_gnn_bn1_g, L0_gnn_bn1_b, L0_gnn_bn1_m, L0_gnn_bn1_v, L0_gnn_conv2_w, L0_gnn_bn2_g, L0_gnn_bn2_b, L0_gnn_bn2_m, L0_gnn_bn2_v, L0_gnn_w_msg, L0_gnn_b_msg, L0_gnn_w_ih, L0_gnn_b_ih, L0_gnn_w_hh, L0_gnn_b_hh), axis=-1)
    x = _layernorm(x + _L1_gnn_ref(x, adj, L1_gnn_W_lin, L1_gnn_b_lin, L1_gnn_W_q, L1_gnn_W_k), axis=-1)
    x = _layernorm(x + _L2_gnn_ref(x, adj), axis=-1)
    x = _layernorm(x + _L3_gnn_ref(x, adj, nodemask, L3_gnn_W, L3_gnn_b), axis=-1)
    return x

_drawn_inputs = setup_inputs


def setup_inputs(seed=0):
    import zlib

    import numpy as np

    out = dict(_drawn_inputs(seed))
    spreads = {'L0_gnn_b_se': (0.0, 0.8),
     'L0_gnn_bn1_g': (1.0, 0.6),
     'L0_gnn_bn1_b': (0.0, 0.381),
     'L0_gnn_bn1_m': (0.0, 0.333),
     'L0_gnn_bn1_v': (1.0, 0.6),
     'L0_gnn_bn2_g': (1.0, 0.2),
     'L0_gnn_bn2_b': (0.0, 0.484),
     'L0_gnn_bn2_m': (0.0, 0.466),
     'L0_gnn_bn2_v': (1.0, 0.6),
     'L0_gnn_b_msg': (0.0, 0.1),
     'L0_gnn_b_ih': (0.0, 0.1),
     'L0_gnn_b_hh': (0.0, 0.1),
     'L1_gnn_b_lin': (0.0, 0.1),
     'L3_gnn_b': (0.0, 0.1)}
    factors = {'L1_gnn_W_q': 7.337, 'L1_gnn_W_k': 6.448}
    for name, (base, spread) in spreads.items():
        noise = np.random.default_rng([zlib.crc32(name.encode()), seed]).standard_normal(out[name].shape)
        drawn = base * np.exp(spread * noise) if base else spread * noise
        out[name] = jnp.asarray(drawn.astype(out[name].dtype))
    for name, factor in factors.items():
        out[name] = (out[name] * factor).astype(out[name].dtype)
    return out
```

```python
from contextlib import ExitStack

import numpy as np
import concourse.bass as bass
from concourse import mybir

F32 = mybir.dt.float32
F32R = mybir.dt.float32r
ALU = mybir.AluOpType
ACT = mybir.ActivationFunctionType

P = 128
B, N = 16, 512
C = N // P
TAPS = 17
HALF = TAPS // 2
PADDED = N + 2 * HALF
LN_EPS = 1e-5
BN_EPS = 1e-5
DEG_EPS = 1e-8
MIN_NORM = 1e-15
SLOPE = 0.01
BALL = 0.996
ATANH_MAX = 1 - 1e-7
SERIES_BELOW = 0.1

W_CONV1, W_CONV2 = 0, P
W_SE = W_CONV2 + TAPS * P
W_MSG = W_SE + P
W_LIN, W_Q, W_K = W_MSG + P, W_MSG + 2 * P, W_MSG + 3 * P
W_IH = W_MSG + 4 * P
W_HH = W_IH + 6 * P
W_SPLIT = W_HH + 3 * P

(G1, B1, M1, V1, G2, B2, M2, V2, BI_R, BI_Z, BI_N, BH_R, BH_Z, BH_N,
 SQ_BIAS, L_A, L_ZA, L_ZC, R_A, R_ZA, R_ZC) = range(21)
N_PAR = 21

EVENTS = (
    "xh xl xcopy sq_ready zl_ready zr_ready stl_ready str_ready h1_ready h1h_ready h1l_ready "
    "msg_added msg_ready xconv_sum xconv_ready xch_ready xcl_ready nmp_ready nmph_ready nmpl_ready "
    "r_ready w_ready gate_t gate_u n_ready gate_d gate_e y_ready "
    "a0_ready a1_01 a1_23 g1_done conv1_done msg_done g_done conv2_done agg0_done gates_done yt_done "
    "ln_stats ln_sums ln_parts ln_eps ln_rstd x1_ready "
    "x1t_done x1t_ready x1th_ready x1tl_ready x_done q_done k_done q_raw k_raw q_ready k_ready x_added xact_ready "
    "asum01 asum23 asum_ready dsum01 dsum23 dsum_ready deg_done deg_read d_zero d_safe d_pow d_mask dinv_ready "
    "dis_eps dis_ready xs_ready agg1_done agg1_ready nat1_done z1_ready "
    "x2_ready "
    "dis_kept ss_ready nrm_pow z_ready oneminus rec_ready ratio_ready ln_ready "
    "w_sq ser1 ser2 ser3 main_f diff_f mix_f f_ready xt_ready agg2_done agg2_ready nat2_done "
    "ssu_ready nu_pow nu_ready tanh_ready rnu_ready g_ready ny_ready nyc_ready rny_ready fac_ready g2_ready z2_ready "
    "x3_ready x3t_done x3t_ready hlin_done hlin_added hs_ready "
    "agg3_done agg3_ready nat3_done dm_ready res_ready res_scaled z3_ready out_ready"
).split()
CHUNK_EVENTS = "dist_done exp_ready att_done sig_ready".split()
DMA_EVENTS = "x_loaded adjf_loaded adjm_loaded adjr_loaded mask_loaded out_stored".split()


def adj_resnorm_kernel(nc, xT_d, adjT_d, mask_d, weights_d, rows_d, params_d, sqmat_d, ident_d, out_d):
    ctx = ExitStack()
    with ctx:
        def sb(name, shape, dt=F32):
            return ctx.enter_context(nc.sbuf_tensor(name, shape, dt))

        def bank(name):
            return ctx.enter_context(nc.psum_tensor(name, [P, N], F32))

        def sem(name):
            return ctx.enter_context(nc.semaphore(name))

        WOUT = sb("WOUT", [P, P])
        WH = sb("WH", [P, W_SPLIT], F32R)
        WL = sb("WL", [P, W_SPLIT], F32R)
        ROWS = sb("ROWS", [P, 3, P])
        PAR = sb("PAR", [P, N_PAR])
        SQMAT = sb("SQMAT", [P, P])
        IDENT = sb("IDENT", [P, P])
        ONES = sb("ONES", [P, 1])
        POW = sb("POW", [P, 2, C])
        VE = sb("VE", [P, 2])
        RS = sb("RS", [P, 2])
        SC = sb("SC", [P, 2])
        MS = sb("MS", [P, 2])
        BI = sb("BI", [P, 2])
        BG = sb("BG", [P, 2])
        NBZ = sb("NBZ", [P, 1])

        X_IN = sb("X_IN", [P, N])
        ADJF = sb("ADJF", [P, C, N])
        ADJM = sb("ADJM", [P, C, N])
        ADJR = sb("ADJR", [P, C, N])
        MASK = sb("MASK", [P, C])

        XT, XH, XL = sb("XT", [P, N]), sb("XH", [P, N], F32R), sb("XL", [P, N], F32R)
        SQ = sb("SQ", [P, N])
        ZL, ZR = sb("ZL", [P, N], F32R), sb("ZR", [P, N], F32R)
        STL, STR = sb("STL", [P, N], F32R), sb("STR", [P, N], F32R)
        H1 = sb("H1", [P, N])
        H1H, H1L = sb("H1H", [P, PADDED], F32R), sb("H1L", [P, PADDED], F32R)
        XCS, XC = sb("XCS", [P, N]), sb("XC", [P, N])
        XCH, XCL = sb("XCH", [P, N], F32R), sb("XCL", [P, N], F32R)
        MSGA, MSG = sb("MSGA", [P, C, P]), sb("MSG", [P, C, P])
        A0 = sb("A0", [P, C, N])
        NMP, NMH, NML = sb("NMP", [P, N]), sb("NMH", [P, N], F32R), sb("NML", [P, N], F32R)
        R, WG, NG = sb("R", [P, N]), sb("WG", [P, N]), sb("NG", [P, N])
        GT, GD, Y = (sb(n, [P, N]) for n in ("GT", "GD", "Y"))
        X1 = sb("X1", [P, C, P])

        X1T, X1H, X1L = sb("X1T", [P, N]), sb("X1H", [P, N], F32R), sb("X1L", [P, N], F32R)
        XA, XX, XS = sb("XA", [P, C, P]), sb("XX", [P, C, P]), sb("XS", [P, C, P])
        QRAW, KRAW, QT, KT = (sb(n, [P, N]) for n in ("QRAW", "KRAW", "QT", "KT"))
        BIG = sb("BIG", [P, 2, C, N])
        SIG, A1 = BIG[:, 0, :, :], BIG[:, 1, :, :]
        W = BIG[:, :, :, :].rearrange("p a c n -> p (a c n)")
        ASUM = sb("ASUM", [P, 3, N])
        DSUM = sb("DSUM", [P, 3, N])
        D = sb("D", [P, 8, C])
        DINV, DIS, DIS_R = sb("DINV", [P, C]), sb("DIS", [P, C]), sb("DIS_R", [P, C])
        AG1, Z1, X2 = sb("AG1", [P, N]), sb("Z1", [P, C, P]), sb("X2", [P, C, P])

        JUNK = sb("JUNK", [P, 2 * C, P], mybir.dt.bfloat16)
        T = sb("T", [P, 32, C])
        XTAN, AG2, Z2, X3 = sb("XTAN", [P, C, P]), sb("AG2", [P, N]), sb("Z2", [P, C, P]), sb("X3", [P, C, P])
        X3T, HL, HS = sb("X3T", [P, N]), sb("HL", [P, C, P]), sb("HS", [P, C, P])
        AG3, RES, Z3 = sb("AG3", [P, N]), sb("RES", [P, C, P]), sb("Z3", [P, C, P])
        DM = sb("DM", [P, C])
        OUT = sb("OUT", [P, C, P])

        ST = sb("ST", [P, 4, C, 6])
        LT = sb("LT", [P, 5, C])
        MEAN = sb("MEAN", [P, 4, C])
        VEPS = sb("VEPS", [P, 4, C])
        RSTD = sb("RSTD", [P, 4, C])

        CONV, F0, F1, C0, C1, K0, K1, K2 = (bank(n) for n in ("CONV", "F0", "F1", "C0", "C1", "K0", "K1", "K2"))
        CB = (C0, C1)

        ev = {n: sem("s_" + n) for n in EVENTS + DMA_EVENTS}
        for n in CHUNK_EVENTS:
            for c in range(C):
                ev[n, c] = sem(f"s_{n}_{c}")
        s_const, s_split, s_prep = sem("s_const"), sem("s_split"), sem("s_prep")
        s_weights, s_conv2w = sem("s_weights"), sem("s_conv2w")
        s_set, s_bn_pow, s_bn = sem("s_set"), sem("s_bn_pow"), sem("s_bn")

        def at(e, t, k):
            return max(0, min(t + k, B)) if isinstance(t, int) else (e.snap(t + k) if k else t)

        def counts(e, t):
            n = {k: at(e, t, k) for k in (1, 0, -1, -2)}
            n = {"f": n[1], "f_prev": n[0], "m": n[0], "m_prev": n[-1], "r": n[-1], "r_prev": n[-2]}
            if e in (nc.vector, nc.gpsimd):
                if isinstance(t, int):
                    n["ln2"] = n["f_prev"] + n["m_prev"] + n["r_prev"] + n["r"]
                    n["ln1"] = n["f_prev"] + n["m"] + n["r_prev"] + n["r"]
                    n["ln3"] = n["f_prev"] + n["m"] + 2 * n["r"]
                    n["ln0"] = n["f"] + n["m"] + 2 * n["r"]
                else:
                    for k, name in ((4, "ln2"), (3, "ln1"), (2, "ln3"), (1, "ln0")):
                        n[name] = e.snap(4 * t - k)
            return n

        def wait(e, name, count, per=1):
            if not isinstance(count, int) or count > 0:
                e.wait_ge(ev[name], count * per)

        def slots(e, body):
            for t in range(3):
                body(t, True, t >= 1, t >= 2)
            with e.Fori(3, B - 1) as t:
                body(t, True, True, True)
            body(B - 1, True, True, True)
            body(B, False, True, True)
            body(B + 1, False, False, True)

        def spread(v):
            return v.unsqueeze(2).to_broadcast([P, C, P])

        def chunked(t):
            return t[:, :].rearrange("p (c n) -> p c n", c=C)

        def cols(t, c):
            return t[:, c * P:(c + 1) * P]

        block = ctx.enter_context(nc.Block())

        @block.sync
        def _(sp):
            sp.dma_start(X_IN[:, :], xT_d[0]).then_inc(ev["x_loaded"], 16)
            sp.dma_start(PAR[:, :], params_d).then_inc(s_const, 16)
            sp.dma_start(SQMAT[:, :], sqmat_d).then_inc(s_const, 16)
            sp.dma_start(IDENT[:, :], ident_d).then_inc(s_const, 16)
            sp.dma_start(ROWS[:, :, :], rows_d).then_inc(s_const, 16)
            sp.dma_start(W[:, 0:W_CONV2], weights_d[:, 0:W_CONV2]).then_inc(s_weights, 16)
            sp.dma_start(W[:, W_SE:], weights_d[:, W_SE:W_SPLIT]).then_inc(s_weights, 16)
            sp.dma_start(WOUT[:, :], weights_d[:, W_SPLIT:]).then_inc(s_weights, 16)
            sp.dma_start(ADJF[:, :, :], adjT_d[0].rearrange("(c p) n -> p c n", p=P)).then_inc(ev["adjf_loaded"], 16)
            sp.dma_start(W[:, W_CONV2:W_SE], weights_d[:, W_CONV2:W_SE]).then_inc(s_conv2w, 16)

            def loads(t, front, mid, rear):
                n = counts(sp, t)
                static = isinstance(t, int)
                if not static or t + 1 < B:
                    nxt = sp.snap(t + 1) if not static else t + 1
                    for name in ("xh", "xl", "xcopy"):
                        wait(sp, name, n["f"])
                    sp.dma_start(X_IN[:, :], xT_d[nxt]).then_inc(ev["x_loaded"], 16)
                    wait(sp, "a0_ready", n["f"])
                    sp.dma_start(ADJF[:, :, :], adjT_d[nxt].rearrange("(c p) n -> p c n", p=P)).then_inc(
                        ev["adjf_loaded"], 16)
                if not static or t < B:
                    wait(sp, "a1_23", n["m"])
                    wait(sp, "dsum01", n["m"])
                    wait(sp, "dsum23", n["m"])
                    sp.dma_start(ADJM[:, :, :], adjT_d[t].rearrange("(c p) n -> p c n", p=P)).then_inc(
                        ev["adjm_loaded"], 16)
                if not static or 0 <= t - 1 < B:
                    last = sp.snap(t - 1) if not static else t - 1
                    wait(sp, "agg3_done", n["r"])
                    sp.dma_start(ADJR[:, :, :], adjT_d[last].rearrange("(c p) n -> p c n", p=P)).then_inc(
                        ev["adjr_loaded"], 16)
                    wait(sp, "dm_ready", n["r"])
                    sp.dma_start(MASK[:, :], mask_d[last]).then_inc(ev["mask_loaded"], 16)
                if rear:
                    done = sp.snap(t - 2) if not static else t - 2
                    wait(sp, "out_ready", n["r"])
                    sp.dma_start(out_d[done].rearrange("(c p) d -> p c d", p=P), OUT[:, :, :]).then_inc(
                        ev["out_stored"], 16)

            slots(sp, loads)
            sp.wait_ge(ev["out_stored"], 16 * B)

        @block.gpsimd
        def _(pool):
            nc.gpsimd.memset(POW[:, 0, :], -0.5).then_inc(s_set, 1)
            nc.gpsimd.memset(POW[:, 1, :], 0.5).then_inc(s_set, 1)
            nc.gpsimd.memset(ONES[:, :], 1.0).then_inc(s_set, 1)
            pool.wait_ge(s_set, 3)
            pool.wait_ge(s_prep, 1)
            nc.gpsimd.tensor_tensor(RS[:, :], VE[:, :], POW[:, 0, 0:2], ALU.pow).then_inc(s_bn_pow, 1)

            def rstd(layer, count):
                wait(pool, "ln_eps", count)
                nc.gpsimd.tensor_tensor(RSTD[:, layer, :], VEPS[:, layer, :], POW[:, 0, :], ALU.pow).then_inc(
                    ev["ln_rstd"], 1)

            def body(t, front, mid, rear):
                n = counts(pool, t)
                if rear:
                    wait(pool, "ss_ready", n["r"])
                    nc.gpsimd.tensor_tensor(T[:, 1, :], T[:, 0, :], POW[:, 1, :], ALU.pow).then_inc(ev["nrm_pow"], 1)
                if mid:
                    wait(pool, "adjm_loaded", n["m"], 16)
                    wait(pool, "deg_done", n["m_prev"])
                    for half, name in ((0, "dsum01"), (1, "dsum23")):
                        nc.gpsimd.tensor_tensor(DSUM[:, half, :], ADJM[:, 2 * half, :], ADJM[:, 2 * half + 1, :],
                                                ALU.add).then_inc(ev[name], 1)
                    wait(pool, "dsum01", n["m"])
                    wait(pool, "dsum23", n["m"])
                    nc.gpsimd.tensor_tensor(DSUM[:, 2, :], DSUM[:, 0, :], DSUM[:, 1, :], ALU.add).then_inc(
                        ev["dsum_ready"], 1)
                if rear:
                    wait(pool, "ssu_ready", n["r"])
                    nc.gpsimd.tensor_tensor(T[:, 17, :], T[:, 16, :], POW[:, 1, :], ALU.pow).then_inc(
                        ev["nu_pow"], 1)
                if mid:
                    for half, name in ((0, "asum01"), (1, "asum23")):
                        wait(pool, ("a1_01", "a1_23")[half], n["m"])
                        nc.gpsimd.tensor_tensor(ASUM[:, half, :], A1[:, 2 * half, :], A1[:, 2 * half + 1, :],
                                                ALU.add).then_inc(ev[name], 1)
                    wait(pool, "asum01", n["m"])
                    wait(pool, "asum23", n["m"])
                    nc.gpsimd.tensor_tensor(ASUM[:, 2, :], ASUM[:, 0, :], ASUM[:, 1, :], ALU.add).then_inc(
                        ev["asum_ready"], 1)
                if rear:
                    rstd(2, n["ln2"])
                if mid:
                    wait(pool, "d_safe", n["m"])
                    nc.gpsimd.tensor_tensor(D[:, 3, :], D[:, 2, :], POW[:, 0, :], ALU.pow).then_inc(ev["d_pow"], 1)
                    wait(pool, "dis_eps", n["m"])
                    wait(pool, "dis_kept", n["r"])
                    nc.gpsimd.tensor_tensor(DIS[:, :], D[:, 5, :], POW[:, 0, :], ALU.pow).then_inc(
                        ev["dis_ready"], 1)
                    rstd(1, n["ln1"])
                if rear:
                    rstd(3, n["ln3"])
                if front:
                    rstd(0, n["ln0"])

            slots(pool, body)

        @block.scalar
        def _(act):
            A = nc.scalar.activation
            act.wait_ge(s_const, 64)

            def row_squares(out, tile, name, lane):
                for c in range(C):
                    last = A(JUNK[:, lane + c, :], tile(c), ACT.Square, accum_out=out[:, c:c + 1])
                last.then_inc(ev[name], 1)

            def body(t, front, mid, rear):
                n = counts(act, t)
                if front:
                    wait(act, "x_loaded", n["f"], 16)
                    wait(act, "gates_done", n["f_prev"])
                    A(XH[:, :], X_IN[:, :], ACT.Copy).then_inc(ev["xh"], 1)
                nc.scalar.preload_act_table_set("natural_log_exp_and_others")
                if rear:
                    wait(act, "x2_ready", n["r"])
                    row_squares(T[:, 0, :], lambda c: X2[:, c, :], "ss_ready", 0)
                if front:
                    wait(act, "g1_done", n["f"])
                    A(SQ[:, :], CONV[:, :], ACT.Square, bias=PAR[:, SQ_BIAS:SQ_BIAS + 1]).then_inc(ev["sq_ready"], 1)
                    wait(act, "conv1_done", n["f"])
                    if isinstance(t, int) and t == 0:
                        act.wait_ge(s_bn, 1)
                    wait(act, "h1l_ready", n["f_prev"])
                    A(H1[:, :], F1[:, :], ACT.Relu, bias=BI[:, 0:1], scale=SC[:, 0:1]).then_inc(ev["h1_ready"], 1)
                if mid:
                    wait(act, "x1t_done", n["m"])
                    wait(act, "k_done", n["m_prev"])
                    A(X1H[:, :], K0[:, :], ACT.Copy).then_inc(ev["x1th_ready"], 1)
                    A(X1T[:, :], K0[:, :], ACT.Copy).then_inc(ev["x1t_ready"], 1)
                if rear:
                    wait(act, "ratio_ready", n["r"])
                    A(T[:, 7, :], T[:, 6, :], ACT.Ln).then_inc(ev["ln_ready"], 1)
                if front:
                    wait(act, "msg_added", n["f"])
                    wait(act, "agg0_done", n["f_prev"])
                    A(MSG[:, :, :], MSGA[:, :, :], ACT.Relu).then_inc(ev["msg_ready"], 1)
                    wait(act, "g_done", n["f"])
                    A(ZL[:, :], CONV[:, :], ACT.Identity, bias=PAR[:, L_ZC:L_ZC + 1],
                      scale=PAR[:, L_ZA:L_ZA + 1]).then_inc(ev["zl_ready"], 1)
                    A(ZR[:, :], CONV[:, :], ACT.Identity, bias=PAR[:, R_ZC:R_ZC + 1],
                      scale=PAR[:, R_ZA:R_ZA + 1]).then_inc(ev["zr_ready"], 1)
                if rear:
                    wait(act, "agg2_done", n["r"])
                    A(AG2[:, :], K1[:, :], ACT.Copy).then_inc(ev["agg2_ready"], 1)
                if mid:
                    wait(act, "q_done", n["m"])
                    wait(act, "k_ready", n["m_prev"])
                    A(QRAW[:, :], K0[:, :], ACT.Copy).then_inc(ev["q_raw"], 1)
                    wait(act, "k_done", n["m"])
                    A(KRAW[:, :], K1[:, :], ACT.Copy).then_inc(ev["k_raw"], 1)
                if front:
                    wait(act, "agg0_done", n["f_prev"])
                    for c in range(C):
                        wait(act, ("dist_done", c), n["f"])
                        A(A0[:, c, :], CB[c % 2][:, :], ACT.Exp).then_inc(ev["exp_ready", c], 1)
                if rear:
                    wait(act, "nat2_done", n["r"])
                    row_squares(T[:, 16, :], lambda c: cols(K2, c), "ssu_ready", C)
                if mid:
                    wait(act, "a1_23", n["m_prev"])
                    for c in range(C):
                        wait(act, ("att_done", c), n["m"])
                        A(SIG[:, c, :], CB[c % 2][:, :], ACT.Sigmoid, scale=float(P) ** -0.5).then_inc(
                            ev["sig_ready", c], 1)
                if rear:
                    wait(act, "nu_ready", n["r"])
                    A(T[:, 19, :], T[:, 18, :], ACT.Tanh).then_inc(ev["tanh_ready"], 1)
                if front:
                    wait(act, "agg0_done", n["f"])
                    A(NMH[:, :], F0[:, :], ACT.Copy).then_inc(ev["nmph_ready"], 1)
                    A(NMP[:, :], F0[:, :], ACT.Copy).then_inc(ev["nmp_ready"], 1)
                if rear:
                    wait(act, "x3t_done", n["r"])
                    A(X3T[:, :], K1[:, :], ACT.Copy).then_inc(ev["x3t_ready"], 1)
                if mid:
                    wait(act, "agg1_done", n["m"])
                    A(AG1[:, :], K0[:, :], ACT.Copy).then_inc(ev["agg1_ready"], 1)
                if front:
                    wait(act, "xconv_sum", n["f"])
                    A(XC[:, :], XCS[:, :], ACT.Relu, bias=BI[:, 1:2]).then_inc(ev["xconv_ready"], 1)
                if rear:
                    wait(act, "agg3_done", n["r"])
                    A(AG3[:, :], K2[:, :], ACT.Copy).then_inc(ev["agg3_ready"], 1)
                if front:
                    wait(act, "gates_done", n["f"])
                    A(R[:, :], F1[:, :], ACT.Sigmoid, bias=BG[:, 0:1]).then_inc(ev["r_ready"], 1)
                    A(WG[:, :], C0[:, :], ACT.Sigmoid, bias=NBZ[:, :], scale=-1.0).then_inc(ev["w_ready"], 1)
                    wait(act, "gate_u", n["f"])
                    A(NG[:, :], GT[:, :], ACT.Tanh, bias=PAR[:, BI_N:BI_N + 1]).then_inc(ev["n_ready"], 1)

            slots(act, body)

        @block.vector
        def _(dve):
            V = nc.vector
            V.memset(H1H[:, :].bitcast(F32), 0.0)
            V.memset(H1L[:, :].bitcast(F32), 0.0).then_inc(s_set, 1)
            dve.wait_ge(s_const, 64)
            V.tensor_scalar(VE[:, 0:1], PAR[:, V1:V1 + 1], BN_EPS, None, ALU.add)
            V.tensor_scalar(VE[:, 1:2], PAR[:, V2:V2 + 1], BN_EPS, None, ALU.add)
            V.tensor_tensor(BG[:, 0:1], PAR[:, BI_R:BI_R + 1], PAR[:, BH_R:BH_R + 1], ALU.add)
            V.tensor_tensor(BG[:, 1:2], PAR[:, BI_Z:BI_Z + 1], PAR[:, BH_Z:BH_Z + 1], ALU.add).then_inc(s_prep, 1)
            dve.wait_ge(s_prep, 1)
            V.tensor_scalar(NBZ[:, :], BG[:, 1:2], -1.0, None, ALU.mult)
            dve.wait_ge(s_bn_pow, 1)
            V.tensor_tensor(SC[:, 0:1], PAR[:, G1:G1 + 1], RS[:, 0:1], ALU.mult)
            V.tensor_tensor(SC[:, 1:2], PAR[:, G2:G2 + 1], RS[:, 1:2], ALU.mult).then_inc(s_prep, 1)
            dve.wait_ge(s_prep, 2)
            V.tensor_tensor(MS[:, 0:1], PAR[:, M1:M1 + 1], SC[:, 0:1], ALU.mult)
            V.tensor_tensor(MS[:, 1:2], PAR[:, M2:M2 + 1], SC[:, 1:2], ALU.mult).then_inc(s_prep, 1)
            dve.wait_ge(s_prep, 3)
            V.tensor_tensor(BI[:, 0:1], PAR[:, B1:B1 + 1], MS[:, 0:1], ALU.subtract)
            V.tensor_tensor(BI[:, 1:2], PAR[:, B2:B2 + 1], MS[:, 1:2], ALU.subtract).then_inc(s_bn, 1)
            dve.wait_ge(s_weights, 48)
            dve.wait_ge(s_conv2w, 16)
            V.tensor_copy(WH[:, :], W).then_inc(s_prep, 1)
            dve.wait_ge(s_prep, 4)
            V.tensor_tensor(WL[:, :], W, WH[:, :].bitcast(F32), ALU.subtract).then_inc(s_split, 1)

            def norm_rows(layer, src, dst, count, done, free=None):
                for c in range(C):
                    last = V.bn_stats(ST[:, layer, c, :], src(c))
                last.then_inc(ev["ln_stats"], 1)
                wait(dve, "ln_stats", count)
                even, odd = (lambda k, h=h: ST[:, layer, :, 3 * h + k] for h in (0, 1))
                V.tensor_tensor(LT[:, 0, :], even(1), odd(1), ALU.add)
                V.tensor_tensor(LT[:, 1, :], even(1), odd(1), ALU.subtract)
                V.tensor_tensor(LT[:, 2, :], even(2), odd(2), ALU.add).then_inc(ev["ln_sums"], 1)
                wait(dve, "ln_sums", count)
                V.tensor_scalar(MEAN[:, layer, :], LT[:, 0, :], 0.5, None, ALU.mult)
                V.scalar_tensor_tensor(LT[:, 3, :], LT[:, 1, :], 0.25, LT[:, 1, :], ALU.mult, ALU.mult)
                V.tensor_scalar(LT[:, 4, :], LT[:, 2, :], 1 / P, LN_EPS, ALU.mult, ALU.add).then_inc(
                    ev["ln_parts"], 1)
                wait(dve, "ln_parts", count)
                V.tensor_tensor(VEPS[:, layer, :], LT[:, 3, :], LT[:, 4, :], ALU.add).then_inc(ev["ln_eps"], 1)
                wait(dve, "ln_rstd", count)
                if free is not None:
                    free()
                for c in range(C):
                    last = V.tensor_scalar(dst[:, c, :], src(c), MEAN[:, layer, c:c + 1], RSTD[:, layer, c:c + 1],
                                           ALU.subtract, ALU.mult)
                last.then_inc(ev[done], 1)

            def body(t, front, mid, rear):
                n = counts(dve, t)

                def small(name, count, ins):
                    ins.then_inc(ev[name], 1)
                    wait(dve, name, count)

                if front:
                    wait(dve, "x_loaded", n["f"], 16)
                    wait(dve, "xh", n["f"])
                    wait(dve, "gates_done", n["f_prev"])
                    V.tensor_tensor(XL[:, :], X_IN[:, :], XH[:, :].bitcast(F32), ALU.subtract).then_inc(ev["xl"], 1)
                    V.tensor_copy(XT[:, :], X_IN[:, :]).then_inc(ev["xcopy"], 1)
                if rear:
                    wait(dve, "dis_ready", n["r"])
                    V.tensor_copy(DIS_R[:, :], DIS[:, :]).then_inc(ev["dis_kept"], 1)
                    r = n["r"]
                    wait(dve, "nrm_pow", r)
                    V.tensor_scalar(T[:, 2, :], T[:, 1, :], MIN_NORM, None, ALU.max)
                    small("z_ready", r, V.tensor_scalar(T[:, 3, :], T[:, 1, :], MIN_NORM, ATANH_MAX,
                                                        ALU.max, ALU.min))
                    small("oneminus", r, V.tensor_scalar(T[:, 4, :], T[:, 3, :], -1.0, 1.0, ALU.mult, ALU.add))
                    small("rec_ready", r, V.reciprocal(T[:, 5, :], T[:, 4, :]))
                    V.scalar_tensor_tensor(T[:, 6, :], T[:, 3, :], 1.0, T[:, 5, :], ALU.add, ALU.mult).then_inc(
                        ev["ratio_ready"], 1)
                    V.reciprocal(T[:, 8, :], T[:, 2, :])
                    V.tensor_scalar(T[:, 14, :], T[:, 3, :], SERIES_BELOW, None, ALU.is_lt)
                    small("w_sq", r, V.tensor_tensor(T[:, 9, :], T[:, 3, :], T[:, 3, :], ALU.mult))
                    small("ser1", r, V.scalar_tensor_tensor(T[:, 10, :], T[:, 9, :], 7 / 5, T[:, 9, :],
                                                            ALU.add, ALU.mult))
                    small("ser2", r, V.scalar_tensor_tensor(T[:, 11, :], T[:, 10, :], 7 / 3, T[:, 9, :],
                                                            ALU.add, ALU.mult))
                    small("ser3", r, V.tensor_scalar(T[:, 13, :], T[:, 11, :], 1 / 7, 1.0, ALU.mult, ALU.add))
                if front:
                    wait(dve, "h1_ready", n["f"])
                    wait(dve, "conv2_done", n["f_prev"])
                    V.tensor_copy(H1H[:, HALF:HALF + N], H1[:, :]).then_inc(ev["h1h_ready"], 1)
                    wait(dve, "h1h_ready", n["f"])
                    V.tensor_tensor(H1L[:, HALF:HALF + N], H1[:, :], H1H[:, HALF:HALF + N].bitcast(F32),
                                    ALU.subtract).then_inc(ev["h1l_ready"], 1)
                if mid:
                    wait(dve, "x1t_ready", n["m"])
                    wait(dve, "k_done", n["m_prev"])
                    V.tensor_tensor(X1L[:, :], X1T[:, :], X1H[:, :].bitcast(F32), ALU.subtract).then_inc(
                        ev["x1tl_ready"], 1)
                if front:
                    wait(dve, "msg_done", n["f"])
                    wait(dve, "msg_ready", n["f_prev"])
                    V.tensor_tensor(MSGA[:, :, :], chunked(F0),
                                    ROWS[:, 0, :].unsqueeze(1).to_broadcast([P, C, P]), ALU.add).then_inc(
                        ev["msg_added"], 1)
                if rear:
                    r = n["r"]
                    wait(dve, "ln_ready", r)
                    small("main_f", r, V.scalar_tensor_tensor(T[:, 22, :], T[:, 7, :], 0.5, T[:, 8, :],
                                                              ALU.mult, ALU.mult))
                    small("diff_f", r, V.tensor_tensor(T[:, 23, :], T[:, 13, :], T[:, 22, :], ALU.subtract))
                    small("mix_f", r, V.tensor_tensor(T[:, 24, :], T[:, 23, :], T[:, 14, :], ALU.mult))
                    small("f_ready", r, V.tensor_tensor(T[:, 25, :], T[:, 22, :], T[:, 24, :], ALU.add))
                    V.tensor_tensor(XTAN[:, :, :], X2[:, :, :], spread(T[:, 25, :]), ALU.mult).then_inc(
                        ev["xt_ready"], 1)
                if front:
                    wait(dve, "zl_ready", n["f"])
                    wait(dve, "zr_ready", n["f"])
                    V.scalar_tensor_tensor(STL[:, :], CONV[:, :], PAR[:, L_A:L_A + 1], ZL[:, :].bitcast(F32),
                                           ALU.mult, ALU.subtract).then_inc(ev["stl_ready"], 1)
                    V.scalar_tensor_tensor(STR[:, :], CONV[:, :], PAR[:, R_A:R_A + 1], ZR[:, :].bitcast(F32),
                                           ALU.mult, ALU.subtract).then_inc(ev["str_ready"], 1)
                if mid:
                    wait(dve, "x_done", n["m"])
                    V.tensor_tensor(XA[:, :, :], chunked(K2),
                                    ROWS[:, 1, :].unsqueeze(1).to_broadcast([P, C, P]), ALU.add).then_inc(
                        ev["x_added"], 1)
                    wait(dve, "q_raw", n["m"])
                    wait(dve, ("att_done", C - 1), n["m_prev"])
                    V.scalar_tensor_tensor(QT[:, :], QRAW[:, :], SLOPE, QRAW[:, :], ALU.mult, ALU.max).then_inc(
                        ev["q_ready"], 1)
                    wait(dve, "k_raw", n["m"])
                    V.scalar_tensor_tensor(KT[:, :], KRAW[:, :], SLOPE, KRAW[:, :], ALU.mult, ALU.max).then_inc(
                        ev["k_ready"], 1)
                    wait(dve, "x_added", n["m"])
                    V.scalar_tensor_tensor(XX[:, :, :], XA[:, :, :], SLOPE, XA[:, :, :], ALU.mult,
                                           ALU.max).then_inc(ev["xact_ready"], 1)
                if front:
                    wait(dve, "adjf_loaded", n["f"], 16)
                    wait(dve, "agg0_done", n["f_prev"])
                    for c in range(C):
                        wait(dve, ("exp_ready", c), n["f"])
                        last = V.tensor_tensor(A0[:, c, :], A0[:, c, :], ADJF[:, c, :], ALU.mult)
                    last.then_inc(ev["a0_ready"], 1)
                if rear:
                    r = n["r"]
                    wait(dve, "nu_pow", r)
                    small("nu_ready", r, V.tensor_scalar(T[:, 18, :], T[:, 17, :], MIN_NORM, None, ALU.max))
                    V.reciprocal(T[:, 20, :], T[:, 18, :]).then_inc(ev["rnu_ready"], 1)
                if mid:
                    wait(dve, "adjm_loaded", n["m"], 16)
                    wait(dve, "agg1_done", n["m_prev"])
                    for c in range(C):
                        wait(dve, ("sig_ready", c), n["m"])
                        last = V.tensor_tensor(A1[:, c, :], SIG[:, c, :], ADJM[:, c, :], ALU.mult)
                        if c % 2:
                            last.then_inc(ev[("a1_01", "a1_23")[c // 2]], 1)
                if rear:
                    wait(dve, "rnu_ready", r)
                    wait(dve, "tanh_ready", r)
                    small("g_ready", r, V.tensor_tensor(T[:, 21, :], T[:, 19, :], T[:, 20, :], ALU.mult))
                    small("ny_ready", r, V.tensor_tensor(T[:, 26, :], T[:, 21, :], T[:, 17, :], ALU.mult))
                    small("nyc_ready", r, V.tensor_scalar(T[:, 27, :], T[:, 26, :], MIN_NORM, None, ALU.max))
                    small("rny_ready", r, V.reciprocal(T[:, 28, :], T[:, 27, :]))
                    small("fac_ready", r, V.tensor_scalar(T[:, 29, :], T[:, 28, :], BALL, 1.0, ALU.mult, ALU.min))
                    small("g2_ready", r, V.tensor_tensor(T[:, 30, :], T[:, 21, :], T[:, 29, :], ALU.mult))
                    for c in range(C):
                        last = V.scalar_tensor_tensor(Z2[:, c, :], cols(K2, c), T[:, 30, c:c + 1], X2[:, c, :],
                                                      ALU.mult, ALU.add)
                    small("z2_ready", r, last)
                    norm_rows(2, lambda c: Z2[:, c, :], X3, n["ln2"], "x3_ready")
                if mid:
                    m = n["m"]
                    wait(dve, "deg_done", m)
                    V.tensor_copy(D[:, 0, :], K0[:, 0:C])
                    small("dis_eps", m, V.tensor_scalar(D[:, 5, :], K0[:, C:2 * C], 1.0, DEG_EPS, ALU.add, ALU.add))
                    small("d_zero", m, V.tensor_scalar(D[:, 1, :], D[:, 0, :], 0.0, None, ALU.is_equal))
                    small("d_safe", m, V.tensor_tensor(D[:, 2, :], D[:, 0, :], D[:, 1, :], ALU.add))
                    small("d_mask", m, V.tensor_scalar(D[:, 4, :], D[:, 1, :], -1.0, 1.0, ALU.mult, ALU.add))
                    wait(dve, "d_pow", m)
                    small("dinv_ready", m, V.tensor_tensor(DINV[:, :], D[:, 3, :], D[:, 4, :], ALU.mult))
                    wait(dve, "xact_ready", m)
                    V.tensor_tensor(XS[:, :, :], XX[:, :, :], spread(DINV[:, :]), ALU.mult).then_inc(
                        ev["xs_ready"], 1)
                if front:
                    wait(dve, "nmp_ready", n["f"])
                    V.tensor_tensor(NML[:, :], NMP[:, :], NMH[:, :].bitcast(F32), ALU.subtract).then_inc(
                        ev["nmpl_ready"], 1)
                if rear:
                    wait(dve, "hlin_done", r)
                    small("hlin_added", r, V.tensor_tensor(
                        HL[:, :, :], chunked(K2), ROWS[:, 2, :].unsqueeze(1).to_broadcast([P, C, P]), ALU.add))
                    V.tensor_tensor(HS[:, :, :], HL[:, :, :], spread(DIS_R[:, :]), ALU.mult).then_inc(
                        ev["hs_ready"], 1)
                if front:
                    wait(dve, "conv2_done", n["f"])
                    V.scalar_tensor_tensor(XCS[:, :], CONV[:, :], SC[:, 1:2], XT[:, :], ALU.mult, ALU.add).then_inc(
                        ev["xconv_sum"], 1)
                if mid:
                    wait(dve, "nat1_done", m)
                    for c in range(C):
                        last = V.scalar_tensor_tensor(Z1[:, c, :], cols(K1, c), DINV[:, c:c + 1], X1[:, c, :],
                                                      ALU.mult, ALU.add)
                    small("z1_ready", m, last)
                if front:
                    wait(dve, "xconv_ready", n["f"])
                    small("xch_ready", n["f"], V.tensor_copy(XCH[:, :], XC[:, :]))
                    V.tensor_tensor(XCL[:, :], XC[:, :], XCH[:, :].bitcast(F32), ALU.subtract).then_inc(
                        ev["xcl_ready"], 1)
                if mid:
                    norm_rows(1, lambda c: Z1[:, c, :], X2, n["ln1"], "x2_ready")
                if rear:
                    wait(dve, "nat3_done", r)
                    wait(dve, "mask_loaded", r, 16)
                    V.tensor_tensor(DM[:, :], DIS_R[:, :], MASK[:, :], ALU.mult).then_inc(ev["dm_ready"], 1)
                    small("res_ready", r, V.tensor_tensor(RES[:, :, :], chunked(K0), HS[:, :, :], ALU.add))
                    wait(dve, "dm_ready", r)
                    small("res_scaled", r, V.tensor_tensor(RES[:, :, :], RES[:, :, :], spread(DM[:, :]), ALU.mult))
                    small("z3_ready", r, V.scalar_tensor_tensor(Z3[:, :, :], RES[:, :, :], 0.0, X3[:, :, :],
                                                                ALU.max, ALU.add))
                if front:
                    f = n["f"]
                    wait(dve, "r_ready", f)
                    small("gate_t", f, V.scalar_tensor_tensor(GT[:, :], F0[:, :], PAR[:, BH_N:BH_N + 1], R[:, :],
                                                              ALU.add, ALU.mult))
                    V.tensor_tensor(GT[:, :], GT[:, :], C1[:, :], ALU.add).then_inc(ev["gate_u"], 1)
                if rear:
                    norm_rows(3, lambda c: Z3[:, c, :], OUT, n["ln3"], "out_ready",
                              free=lambda: wait(dve, "out_stored", n["r_prev"], 16))
                if front:
                    wait(dve, "n_ready", f)
                    small("gate_d", f, V.tensor_tensor(GD[:, :], NG[:, :], XT[:, :], ALU.subtract))
                    wait(dve, "w_ready", f)
                    small("gate_e", f, V.tensor_tensor(GD[:, :], GD[:, :], WG[:, :], ALU.mult))
                    V.scalar_tensor_tensor(Y[:, :], XT[:, :], 2.0, GD[:, :], ALU.mult, ALU.add).then_inc(
                        ev["y_ready"], 1)
                    wait(dve, "yt_done", f)
                    norm_rows(0, lambda c: cols(CONV, c), X1, n["ln0"], "x1_ready")

            slots(dve, body)

        @block.tensor
        def _(pe):
            mm = nc.tensor.matmul

            def product(out, terms):
                k = 0
                for wgt, mov in terms:
                    for i, j in ((0, 0), (0, 1), (1, 0)):
                        last = mm(out, wgt[i], mov[j], start=(k == 0), stop=(k == 3 * len(terms) - 1))
                        k += 1
                return last

            def weight(at_col):
                return WH[:, at_col:at_col + P], WL[:, at_col:at_col + P]

            def transposed(out, tile):
                for c in range(C):
                    last = nc.tensor.transpose(cols(out, c), tile(c), IDENT[:, :])
                return last

            def aggregate(out, rows, chunks):
                for c in range(C):
                    last = mm(out[:, :], rows[:, c, :], chunks[:, c, :], start=(c == 0), stop=(c == C - 1))
                return last

            pe.wait_ge(s_const, 64)
            pe.wait_ge(s_split, 1)
            pe.wait_ge(s_set, 4)
            pe.wait_ge(s_weights, 48)

            def body(t, front, mid, rear):
                n = counts(pe, t)
                f, m, r = n["f"], n["m"], n["r"]
                xt = (XH[:, :], XL[:, :])
                x1t = (X1H[:, :], X1L[:, :])

                def taps(a, b):
                    for k in range(a, b):
                        for i, (w, h) in enumerate(((WH, H1H), (WH, H1L), (WL, H1H))):
                            last = mm(CONV[:, :], w[:, W_CONV2 + k * P:W_CONV2 + (k + 1) * P], h[:, k:k + N],
                                      start=(k == 0 and i == 0), stop=(k == TAPS - 1 and i == 2))
                    return last

                if front:
                    wait(pe, "xl", f)
                    wait(pe, "x1_ready", n["f_prev"])
                    product(CONV[:, :], [(weight(W_SE), xt)]).then_inc(ev["g1_done"], 1)
                    wait(pe, "r_ready", n["f_prev"])
                    product(F1[:, :], [(weight(W_CONV1), xt)]).then_inc(ev["conv1_done"], 1)
                if mid:
                    wait(pe, "x1_ready", m)
                    wait(pe, "res_ready", n["r_prev"])
                    transposed(K0, lambda c: X1[:, c, :]).then_inc(ev["x1t_done"], 1)
                if front:
                    wait(pe, "gate_t", n["f_prev"])
                    for c in range(C):
                        last = product(cols(F0, c), [((cols(XH, c), cols(XL, c)), weight(W_MSG))])
                    last.then_inc(ev["msg_done"], 1)
                    wait(pe, "sq_ready", f)
                    mm(CONV[:, :], SQMAT[:, :], SQ[:, :], start=False, stop=True, skip_group_check=True).then_inc(
                        ev["g_done"], 1)
                if rear:
                    wait(pe, "xt_ready", r)
                    wait(pe, "adjr_loaded", r, 16)
                    wait(pe, "z1_ready", n["m_prev"])
                    aggregate(K1, XTAN, ADJR).then_inc(ev["agg2_done"], 1)
                if mid:
                    wait(pe, "x1tl_ready", m)
                    wait(pe, "x1th_ready", m)
                    wait(pe, "agg3_ready", n["r_prev"])
                    for c in range(C):
                        last = product(cols(K2, c), [((cols(X1H, c), cols(X1L, c)), weight(W_LIN))])
                    last.then_inc(ev["x_done"], 1)
                    product(K0[:, :], [(weight(W_Q), x1t)]).then_inc(ev["q_done"], 1)
                    wait(pe, "agg2_ready", r)
                    product(K1[:, :], [(weight(W_K), x1t)]).then_inc(ev["k_done"], 1)
                if front:
                    wait(pe, "stl_ready", f)
                    wait(pe, "str_ready", f)
                    for c in range(C):
                        if c < 2:
                            wait(pe, ("w_ready", "gate_u")[c], n["f_prev"])
                        else:
                            wait(pe, ("exp_ready", c - 2), f)
                        mm(CB[c % 2][:, :], cols(STL, c), STR[:, :], start=True, stop=True).then_inc(
                            ev["dist_done", c], 1)
                    wait(pe, "h1l_ready", f)
                    taps(0, 3)
                if rear:
                    wait(pe, "agg2_ready", r)
                    wait(pe, "x_added", m)
                    transposed(K2, lambda c: cols(AG2, c)).then_inc(ev["nat2_done"], 1)
                if mid:
                    wait(pe, "q_ready", m)
                    wait(pe, "k_ready", m)
                    for c in range(C):
                        wait(pe, ("exp_ready", c + 2) if c < 2 else ("sig_ready", c - 2), f if c < 2 else m)
                        mm(CB[c % 2][:, :], cols(KT, c), QT[:, :], start=True, stop=True).then_inc(
                            ev["att_done", c], 1)
                if front:
                    taps(3, 6)
                    wait(pe, "msg_ready", f)
                    wait(pe, "a0_ready", f)
                    aggregate(F0, MSG, A0).then_inc(ev["agg0_done"], 1)
                    taps(6, 8)
                if mid:
                    wait(pe, "asum_ready", m)
                    wait(pe, "dsum_ready", m)
                    for c in range(C):
                        mm(K0[:, c:c + 1], cols(ASUM[:, 2, :], c), ONES[:, :], start=True, stop=True)
                    for c in range(C):
                        last = mm(K0[:, C + c:C + c + 1], cols(DSUM[:, 2, :], c), ONES[:, :], start=True, stop=True)
                    last.then_inc(ev["deg_done"], 1)
                if front:
                    taps(8, 13)
                if rear:
                    wait(pe, "x3_ready", r)
                    wait(pe, "k_raw", m)
                    transposed(K1, lambda c: X3[:, c, :]).then_inc(ev["x3t_done"], 1)
                if front:
                    taps(13, 14)
                if rear:
                    wait(pe, "x3t_ready", r)
                    wait(pe, "z2_ready", r)
                    for c in range(C):
                        last = mm(cols(K2, c), cols(X3T, c), WOUT[:, :], start=True, stop=True)
                    last.then_inc(ev["hlin_done"], 1)
                if mid:
                    wait(pe, "xs_ready", m)
                    aggregate(K0, XS, A1).then_inc(ev["agg1_done"], 1)
                if front:
                    taps(14, TAPS).then_inc(ev["conv2_done"], 1)
                if mid:
                    wait(pe, "agg1_ready", m)
                    wait(pe, "x3t_ready", r)
                    transposed(K1, lambda c: cols(AG1, c)).then_inc(ev["nat1_done"], 1)
                if rear:
                    wait(pe, "hs_ready", r)
                    aggregate(K2, HS, ADJR).then_inc(ev["agg3_done"], 1)
                if front:
                    wait(pe, "nmpl_ready", f)
                    wait(pe, "nmph_ready", f)
                    wait(pe, ("sig_ready", 2), m)
                    wait(pe, ("sig_ready", 3), m)
                    xc, nm = (XCH[:, :], XCL[:, :]), (NMH[:, :], NML[:, :])
                    product(F0[:, :], [(weight(W_HH + 2 * P), xt)])
                    wait(pe, "xcl_ready", f)
                    for out, g in ((F1, 0), (C0, 1)):
                        product(out[:, :], [(weight(W_HH + g * P), xt), (weight(W_IH + (3 + g) * P), nm),
                                            (weight(W_IH + g * P), xc)])
                    product(C1[:, :], [(weight(W_IH + 5 * P), nm), (weight(W_IH + 2 * P), xc)]).then_inc(
                        ev["gates_done"], 1)
                if rear:
                    wait(pe, "agg3_ready", r)
                    wait(pe, "agg1_ready", m)
                    transposed(K0, lambda c: cols(AG3, c)).then_inc(ev["nat3_done"], 1)
                if front:
                    wait(pe, "y_ready", f)
                    wait(pe, "xconv_sum", f)
                    transposed(CONV, lambda c: cols(Y, c)).then_inc(ev["yt_done"], 1)

            slots(pe, body)


def packed(i):
    t = lambda a: np.asarray(a).T
    zeros = np.zeros
    w_se = zeros((P, P), np.float32)
    for g in range(3):
        w_se[:, 5 * g:5 * g + 3] = t(i["L0_gnn_w_se"])
    conv2 = np.asarray(i["L0_gnn_conv2_w"]).transpose(1, 2, 0).reshape(P, TAPS * P)
    w_ih = np.asarray(i["L0_gnn_w_ih"])
    weights = np.concatenate(
        [t(i["L0_gnn_conv1_w"][:, :, 0]), conv2, w_se, t(i["L0_gnn_w_msg"]), i["L1_gnn_W_lin"], i["L1_gnn_W_q"],
         i["L1_gnn_W_k"], t(w_ih[:, :P]), t(w_ih[:, P:]), t(i["L0_gnn_w_hh"]), t(i["L3_gnn_W"])], axis=1)
    rows = np.broadcast_to(np.stack([i["L0_gnn_b_msg"], i["L1_gnn_b_lin"], i["L3_gnn_b"]]), (P, 3, P))
    par = zeros((P, N_PAR), np.float32)
    for k, name in enumerate(("bn1_g", "bn1_b", "bn1_m", "bn1_v", "bn2_g", "bn2_b", "bn2_m", "bn2_v")):
        par[:, k] = i["L0_gnn_" + name]
    for k, name in ((BI_R, "b_ih"), (BH_R, "b_hh")):
        par[:, k:k + 3] = t(np.asarray(i["L0_gnn_" + name]).reshape(3, P))
    sqmat = zeros((P, P), np.float32)
    par[0:3, SQ_BIAS] = i["L0_gnn_b_se"]
    par[3, SQ_BIAS] = 1
    left, right = (1, 1, 1, 0, 1), (2, 2, 2, 1, 0)
    for g in range(3):
        s = slice(5 * g, 5 * g + 5)
        par[s, L_A], par[s, R_A] = left, right
        for rest, a, za, zc, one in ((g == 1, left, L_ZA, L_ZC, 3), (g == 2, right, R_ZA, R_ZC, 4)):
            if rest:
                par[s, za] = a
            else:
                par[5 * g + one, zc] = -1
        sqmat[3, 5 * g:5 * g + 3] = i["L0_gnn_b_se"]
        sqmat[0:3, 5 * g + 3:5 * g + 5] = -1
    c = np.ascontiguousarray
    return {
        "xT": c(np.asarray(i["x"]).transpose(0, 2, 1)), "adjT": c(np.asarray(i["adj"]).transpose(0, 2, 1)),
        "mask": c(np.asarray(i["nodemask"]).reshape(B, C, P).transpose(0, 2, 1)), "weights": c(weights),
        "rows": c(rows), "params": par, "sqmat": sqmat, "ident": np.eye(P, dtype=np.float32),
    }


def kernel(**inputs):
    import concourse.bacc as bacc
    from concourse.bass_utils import run_bass_kernel_spmd

    arrays = packed(inputs)
    nc = bacc.Bacc("TRN2", target_bir_lowering=False, num_devices=1)
    args = [nc.dram_tensor("in_" + k, a.shape, mybir.dt.from_np(a.dtype), kind="ExternalInput").ap()
            for k, a in arrays.items()]
    out = nc.dram_tensor("out", (B, N, P), F32, kind="ExternalOutput").ap()
    adj_resnorm_kernel(nc, *args, out)
    got = run_bass_kernel_spmd(nc, [{"in_" + k: a for k, a in arrays.items()}], core_ids=[0])
    return got.results[0]["out"]
```

```python
from contextlib import ExitStack

import numpy as np
import concourse.bass as bass
from concourse import mybir

F32 = mybir.dt.float32
F32R = mybir.dt.float32r
ALU = mybir.AluOpType
ACT = mybir.ActivationFunctionType

P = 128
B, N = 16, 512
C = N // P
TAPS = 17
HALF = TAPS // 2
PADDED = N + 2 * HALF
LN_EPS = 1e-5
BN_EPS = 1e-5
DEG_EPS = 1e-8
MIN_NORM = 1e-15
SLOPE = 0.01
BALL = 0.996
ATANH_MAX = 1 - 1e-7
SERIES_BELOW = 0.1

W_CONV1, W_CONV2 = 0, P
W_SE = W_CONV2 + TAPS * P
W_MSG = W_SE + P
W_LIN, W_Q, W_K = W_MSG + P, W_MSG + 2 * P, W_MSG + 3 * P
W_IH = W_MSG + 4 * P
W_HH = W_IH + 6 * P
W_SPLIT = W_HH + 3 * P

(G1, B1, M1, V1, G2, B2, M2, V2, BI_R, BI_Z, BI_N, BH_R, BH_Z, BH_N,
 SQ_BIAS, L_A, L_ZA, L_ZC, R_A, R_ZA, R_ZC) = range(21)
N_PAR = 21

EVENTS = (
    "xh xl xcopy sq_ready zl_ready zr_ready stl_ready str_ready h1_ready h1h_ready h1l_ready "
    "msg_added msg_ready xconv_sum xconv_ready xch_ready xcl_ready nmp_ready nmph_ready nmpl_ready "
    "r_ready w_ready gate_t gate_u n_ready gate_d gate_e y_ready x_used gater_done "
    "a0_ready a1_01 a1_23 g1_done conv1_done msg_done g_done conv2_done agg0_done gates_done yt_done "
    "ln_stats ln_sums ln_parts ln_eps ln_rstd x1_ready "
    "x1t_done x1t_ready x1th_ready x1tl_ready x_done q_done k_done q_raw k_raw q_ready k_ready x_added xact_ready "
    "asum01 asum23 asum_ready dsum01 dsum23 dsum_ready deg_done deg_read d_zero d_safe d_pow d_mask dinv_ready "
    "dis_eps dis_ready xs_ready agg1_done agg1_ready nat1_done z1_ready "
    "x2_ready "
    "dis_kept ss_ready nrm_pow z_ready oneminus rec_ready ratio_ready ln_ready "
    "w_sq ser1 ser2 ser3 main_f diff_f mix_f f_ready xt_ready agg2_done agg2_ready nat2_done "
    "ssu_ready nu_pow nu_ready tanh_ready rnu_ready g_ready ny_ready nyc_ready rny_ready fac_ready g2_ready z2_ready "
    "x3_ready x3t_done x3t_ready hlin_done hlin_added hs_ready "
    "agg3_done agg3_ready nat3_done dm_ready res_ready res_scaled z3_ready out_ready"
).split()
CHUNK_EVENTS = "dist_done exp_ready att_done sig_ready".split()
DMA_EVENTS = "x_loaded adjf_loaded adjm_loaded adjr_loaded mask_loaded out_stored".split()


def adj_resnorm_kernel(nc, xT_d, adjT_d, mask_d, weights_d, rows_d, params_d, sqmat_d, ident_d, out_d):
    ctx = ExitStack()
    with ctx:
        def sb(name, shape, dt=F32):
            return ctx.enter_context(nc.sbuf_tensor(name, shape, dt))

        def bank(name):
            return ctx.enter_context(nc.psum_tensor(name, [P, N], F32))

        def sem(name):
            return ctx.enter_context(nc.semaphore(name))

        WOUT = sb("WOUT", [P, P])
        WH = sb("WH", [P, W_SPLIT], F32R)
        WL = sb("WL", [P, W_SPLIT], F32R)
        ROWS = sb("ROWS", [P, 3, P])
        PAR = sb("PAR", [P, N_PAR])
        SQMAT = sb("SQMAT", [P, P])
        IDENT = sb("IDENT", [P, P])
        ONES = sb("ONES", [P, 1])
        POW = sb("POW", [P, 2, C])
        VE = sb("VE", [P, 2])
        RS = sb("RS", [P, 2])
        SC = sb("SC", [P, 2])
        MS = sb("MS", [P, 2])
        BI = sb("BI", [P, 2])
        BG = sb("BG", [P, 2])
        NBZ = sb("NBZ", [P, 1])

        X_IN = sb("X_IN", [P, N])
        ADJF = sb("ADJF", [P, C, N])
        ADJM = sb("ADJM", [P, C, N])
        ADJR = sb("ADJR", [P, C, N])
        MASK = sb("MASK", [P, C])

        XT, XH, XL = sb("XT", [P, N]), sb("XH", [P, N], F32R), sb("XL", [P, N], F32R)
        SQ = sb("SQ", [P, N])
        ZL, ZR = sb("ZL", [P, N], F32R), sb("ZR", [P, N], F32R)
        STL, STR = sb("STL", [P, N], F32R), sb("STR", [P, N], F32R)
        H1 = sb("H1", [P, N])
        H1H, H1L = sb("H1H", [P, PADDED], F32R), sb("H1L", [P, PADDED], F32R)
        XCS, XC = sb("XCS", [P, N]), sb("XC", [P, N])
        XCH, XCL = sb("XCH", [P, N], F32R), sb("XCL", [P, N], F32R)
        MSGA, MSG = sb("MSGA", [P, C, P]), sb("MSG", [P, C, P])
        A0 = sb("A0", [P, C, N])
        NMP, NMH, NML = sb("NMP", [P, N]), sb("NMH", [P, N], F32R), sb("NML", [P, N], F32R)
        R, WG, NG = sb("R", [P, N]), sb("WG", [P, N]), sb("NG", [P, N])
        GT, GD, Y = (sb(n, [P, N]) for n in ("GT", "GD", "Y"))
        X1 = sb("X1", [P, C, P])

        X1T, X1H, X1L = sb("X1T", [P, N]), sb("X1H", [P, N], F32R), sb("X1L", [P, N], F32R)
        XA, XX, XS = sb("XA", [P, C, P]), sb("XX", [P, C, P]), sb("XS", [P, C, P])
        QRAW, KRAW, QT, KT = (sb(n, [P, N]) for n in ("QRAW", "KRAW", "QT", "KT"))
        BIG = sb("BIG", [P, 2, C, N])
        SIG, A1 = BIG[:, 0, :, :], BIG[:, 1, :, :]
        W = BIG[:, :, :, :].rearrange("p a c n -> p (a c n)")
        ASUM = sb("ASUM", [P, 3, N])
        DSUM = sb("DSUM", [P, 3, N])
        D = sb("D", [P, 8, C])
        DINV, DIS, DIS_R = sb("DINV", [P, C]), sb("DIS", [P, C]), sb("DIS_R", [P, C])
        AG1, Z1, X2 = sb("AG1", [P, N]), sb("Z1", [P, C, P]), sb("X2", [P, C, P])

        JUNK = sb("JUNK", [P, 2 * C, P], mybir.dt.bfloat16)
        T = sb("T", [P, 32, C])
        XTAN, AG2, Z2, X3 = sb("XTAN", [P, C, P]), sb("AG2", [P, N]), sb("Z2", [P, C, P]), sb("X3", [P, C, P])
        X3T, HL, HS = sb("X3T", [P, N]), sb("HL", [P, C, P]), sb("HS", [P, C, P])
        AG3, RES, Z3 = sb("AG3", [P, N]), sb("RES", [P, C, P]), sb("Z3", [P, C, P])
        DM = sb("DM", [P, C])
        OUT = sb("OUT", [P, C, P])

        ST = sb("ST", [P, 4, C, 6])
        LT = sb("LT", [P, 4, 5, C])
        MEAN = sb("MEAN", [P, 4, C])
        VEPS = sb("VEPS", [P, 4, C])
        RSTD = sb("RSTD", [P, 4, C])

        CONV, F0, F1, C0, C1, K0, K1, K2 = (bank(n) for n in ("CONV", "F0", "F1", "C0", "C1", "K0", "K1", "K2"))
        CB = (C0, C1)

        ev = {n: sem("s_" + n) for n in EVENTS + DMA_EVENTS}
        for n in CHUNK_EVENTS:
            for c in range(C):
                ev[n, c] = sem(f"s_{n}_{c}")
        s_const, s_split, s_prep = sem("s_const"), sem("s_split"), sem("s_prep")
        s_weights, s_conv2w = sem("s_weights"), sem("s_conv2w")
        s_set, s_bn_pow, s_bn = sem("s_set"), sem("s_bn_pow"), sem("s_bn")

        def at(e, t, k):
            return max(0, min(t + k, B)) if isinstance(t, int) else (e.snap(t + k) if k else t)

        def counts(e, t):
            n = {k: at(e, t, k) for k in (2, 1, 0, -1, -2, -3)}
            n = {"f_next": n[2], "f": n[1], "f_prev": n[0], "m": n[0], "m_prev": n[-1], "r": n[-1],
                 "r_prev": n[-2], "l": n[-2], "l_prev": n[-3]}
            if e in (nc.vector, nc.gpsimd):
                if isinstance(t, int):
                    n["ln0"] = n["l_prev"] + n["m"] + n["m_prev"] + n["r_prev"]
                    n["ln3"] = n["l"] + n["m"] + n["m_prev"] + n["r_prev"]
                    n["ln2"] = n["l"] + n["m"] + n["m_prev"] + n["r"]
                    n["ln1"] = n["l"] + 2 * n["m"] + n["r"]
                else:
                    for k, name in ((6, "ln0"), (5, "ln3"), (4, "ln2"), (3, "ln1")):
                        n[name] = e.snap(4 * t - k)
            return n

        def slots(e, body):
            for t in range(4):
                body(t, True, t >= 1, t >= 2, t >= 3)
            with e.Fori(4, B - 1) as t:
                body(t, True, True, True, True)
            body(B - 1, True, True, True, True)
            body(B, False, True, True, True)
            body(B + 1, False, False, True, True)
            body(B + 2, False, False, False, True)

        def spread(v):
            return v.unsqueeze(2).to_broadcast([P, C, P])

        def chunked(t):
            return t[:, :].rearrange("p (c n) -> p c n", c=C)

        def cols(t, c):
            return t[:, c * P:(c + 1) * P]

        block = ctx.enter_context(nc.Block())

        @block.sync
        def _(sp):
            sp.dma_start(X_IN[:, :], xT_d[0]).then_inc(ev["x_loaded"], 16)
            sp.dma_start(PAR[:, :], params_d).then_inc(s_const, 16)
            sp.dma_start(SQMAT[:, :], sqmat_d).then_inc(s_const, 16)
            sp.dma_start(IDENT[:, :], ident_d).then_inc(s_const, 16)
            sp.dma_start(ROWS[:, :, :], rows_d).then_inc(s_const, 16)
            sp.dma_start(W[:, 0:W_CONV2], weights_d[:, 0:W_CONV2]).then_inc(s_weights, 16)
            sp.dma_start(W[:, W_SE:], weights_d[:, W_SE:W_SPLIT]).then_inc(s_weights, 16)
            sp.dma_start(WOUT[:, :], weights_d[:, W_SPLIT:]).then_inc(s_weights, 16)
            sp.dma_start(ADJF[:, :, :], adjT_d[0].rearrange("(c p) n -> p c n", p=P)).then_inc(ev["adjf_loaded"], 16)
            sp.dma_start(W[:, W_CONV2:W_SE], weights_d[:, W_CONV2:W_SE]).then_inc(s_conv2w, 16)

            def loads(t, front, mid, rear, late):
                n = counts(sp, t)
                static = isinstance(t, int)
                if not static or t + 1 < B:
                    nxt = sp.snap(t + 1) if not static else t + 1
                    sp.wait_ge(ev["xh"], n["f"])
                    sp.wait_ge(ev["xl"], n["f"])
                    sp.wait_ge(ev["xcopy"], n["f"])
                    sp.dma_start(X_IN[:, :], xT_d[nxt]).then_inc(ev["x_loaded"], 16)
                    sp.wait_ge(ev["a0_ready"], n["f"])
                    sp.dma_start(ADJF[:, :, :], adjT_d[nxt].rearrange("(c p) n -> p c n", p=P)).then_inc(
                        ev["adjf_loaded"], 16)
                if not static or t < B:
                    sp.wait_ge(ev["a1_23"], n["m"])
                    sp.wait_ge(ev["dsum01"], n["m"])
                    sp.wait_ge(ev["dsum23"], n["m"])
                    sp.dma_start(ADJM[:, :, :], adjT_d[t].rearrange("(c p) n -> p c n", p=P)).then_inc(
                        ev["adjm_loaded"], 16)
                if not static or 0 <= t - 1 < B:
                    last = sp.snap(t - 1) if not static else t - 1
                    sp.wait_ge(ev["agg3_done"], n["r"])
                    sp.dma_start(ADJR[:, :, :], adjT_d[last].rearrange("(c p) n -> p c n", p=P)).then_inc(
                        ev["adjr_loaded"], 16)
                    sp.wait_ge(ev["dm_ready"], n["r"])
                    sp.dma_start(MASK[:, :], mask_d[last]).then_inc(ev["mask_loaded"], 16)
                if late:
                    done = sp.snap(t - 3) if not static else t - 3
                    sp.wait_ge(ev["out_ready"], n["l"])
                    sp.dma_start(out_d[done].rearrange("(c p) d -> p c d", p=P), OUT[:, :, :]).then_inc(
                        ev["out_stored"], 16)

            slots(sp, loads)
            sp.wait_ge(ev["out_stored"], 16 * B)

        @block.gpsimd
        def _(pool):
            nc.gpsimd.memset(POW[:, 0, :], -0.5).then_inc(s_set, 1)
            nc.gpsimd.memset(POW[:, 1, :], 0.5).then_inc(s_set, 1)
            nc.gpsimd.memset(ONES[:, :], 1.0).then_inc(s_set, 1)
            pool.wait_ge(s_set, 3)
            pool.wait_ge(s_prep, 1)
            nc.gpsimd.tensor_tensor(RS[:, :], VE[:, :], POW[:, 0, 0:2], ALU.pow).then_inc(s_bn_pow, 1)

            def rstd(layer, count):
                pool.wait_ge(ev["ln_eps"], count)
                nc.gpsimd.tensor_tensor(RSTD[:, layer, :], VEPS[:, layer, :], POW[:, 0, :], ALU.pow).then_inc(
                    ev["ln_rstd"], 1)

            def body(t, front, mid, rear, late):
                n = counts(pool, t)
                if rear:
                    pool.wait_ge(ev["ss_ready"], n["r"])
                    nc.gpsimd.tensor_tensor(T[:, 1, :], T[:, 0, :], POW[:, 1, :], ALU.pow).then_inc(ev["nrm_pow"], 1)
                if mid:
                    rstd(0, n["ln0"])
                    pool.wait_ge(ev["adjm_loaded"], 16 * n["m"])
                    pool.wait_ge(ev["deg_done"], n["m_prev"])
                    for half, name in ((0, "dsum01"), (1, "dsum23")):
                        nc.gpsimd.tensor_tensor(DSUM[:, half, :], ADJM[:, 2 * half, :], ADJM[:, 2 * half + 1, :],
                                                ALU.add).then_inc(ev[name], 1)
                    pool.wait_ge(ev["dsum01"], n["m"])
                    pool.wait_ge(ev["dsum23"], n["m"])
                    nc.gpsimd.tensor_tensor(DSUM[:, 2, :], DSUM[:, 0, :], DSUM[:, 1, :], ALU.add).then_inc(
                        ev["dsum_ready"], 1)
                if late:
                    rstd(3, n["ln3"])
                if rear:
                    pool.wait_ge(ev["ssu_ready"], n["r"])
                    nc.gpsimd.tensor_tensor(T[:, 17, :], T[:, 16, :], POW[:, 1, :], ALU.pow).then_inc(
                        ev["nu_pow"], 1)
                    rstd(2, n["ln2"])
                if mid:
                    pool.wait_ge(ev["a1_01"], n["m"])
                    nc.gpsimd.tensor_tensor(ASUM[:, 0, :], A1[:, 0, :], A1[:, 1, :], ALU.add).then_inc(
                        ev["asum01"], 1)
                    pool.wait_ge(ev["d_safe"], n["m"])
                    nc.gpsimd.tensor_tensor(D[:, 3, :], D[:, 2, :], POW[:, 0, :], ALU.pow).then_inc(ev["d_pow"], 1)
                    pool.wait_ge(ev["dis_eps"], n["m"])
                    pool.wait_ge(ev["dis_kept"], n["r"])
                    nc.gpsimd.tensor_tensor(DIS[:, :], D[:, 5, :], POW[:, 0, :], ALU.pow).then_inc(
                        ev["dis_ready"], 1)
                    rstd(1, n["ln1"])

            slots(pool, body)

        @block.scalar
        def _(act):
            A = nc.scalar.activation
            act.wait_ge(s_const, 64)

            def row_squares(out, tile, name, lane):
                for c in range(C):
                    last = A(JUNK[:, lane + c, :], tile(c), ACT.Square, accum_out=out[:, c:c + 1])
                last.then_inc(ev[name], 1)

            def leading_x(count, previous):
                act.wait_ge(ev["x_loaded"], 16 * count)
                act.wait_ge(ev["x_used"], previous)
                A(XH[:, :], X_IN[:, :], ACT.Copy).then_inc(ev["xh"], 1)

            leading_x(1, 0)

            def body(t, front, mid, rear, late):
                n = counts(act, t)

                def exps(a, b):
                    for c in range(a, b):
                        act.wait_ge(ev["dist_done", c], n["f"])
                        A(A0[:, c, :], CB[c % 2][:, :], ACT.Exp).then_inc(ev["exp_ready", c], 1)

                def sigmoids(a, b):
                    for c in range(a, b):
                        act.wait_ge(ev["att_done", c], n["m"])
                        A(SIG[:, c, :], CB[c % 2][:, :], ACT.Sigmoid, scale=float(P) ** -0.5).then_inc(
                            ev["sig_ready", c], 1)

                if front:
                    act.wait_ge(ev["g1_done"], n["f"])
                    A(SQ[:, :], F1[:, :], ACT.Square, bias=PAR[:, SQ_BIAS:SQ_BIAS + 1]).then_inc(ev["sq_ready"], 1)
                if front:
                    act.wait_ge(ev["conv1_done"], n["f"])
                    if isinstance(t, int) and t == 0:
                        act.wait_ge(s_bn, 1)
                    act.wait_ge(ev["h1l_ready"], n["f_prev"])
                    act.wait_ge(ev["conv2_done"], n["f_prev"])
                    A(H1H[:, HALF:HALF + N], F0[:, :], ACT.Relu, bias=BI[:, 0:1], scale=SC[:, 0:1]).then_inc(
                        ev["h1h_ready"], 1)
                    A(H1[:, :], F0[:, :], ACT.Relu, bias=BI[:, 0:1], scale=SC[:, 0:1]).then_inc(ev["h1_ready"], 1)
                if mid:
                    act.wait_ge(ev["gate_u"], n["m"])
                    A(NG[:, :], GT[:, :], ACT.Tanh, bias=PAR[:, BI_N:BI_N + 1]).then_inc(ev["n_ready"], 1)
                nc.scalar.preload_act_table_set("natural_log_exp_and_others")
                if rear:
                    act.wait_ge(ev["x2_ready"], n["r"])
                    row_squares(T[:, 0, :], lambda c: X2[:, c, :], "ss_ready", 0)
                if front:
                    act.wait_ge(ev["g_done"], n["f"])
                    A(ZL[:, :], F1[:, :], ACT.Identity, bias=PAR[:, L_ZC:L_ZC + 1],
                      scale=PAR[:, L_ZA:L_ZA + 1]).then_inc(ev["zl_ready"], 1)
                    A(ZR[:, :], F1[:, :], ACT.Identity, bias=PAR[:, R_ZC:R_ZC + 1],
                      scale=PAR[:, R_ZA:R_ZA + 1]).then_inc(ev["zr_ready"], 1)
                    act.wait_ge(ev["msg_added"], n["f"])
                    act.wait_ge(ev["agg0_done"], n["f_prev"])
                    A(MSG[:, :, :], MSGA[:, :, :], ACT.Relu).then_inc(ev["msg_ready"], 1)
                    exps(0, 2)
                if rear:
                    act.wait_ge(ev["ratio_ready"], n["r"])
                    A(T[:, 7, :], T[:, 6, :], ACT.Ln).then_inc(ev["ln_ready"], 1)
                if front:
                    exps(2, C)
                nc.scalar.preload_act_table_set("sigmoid_and_others")
                if rear:
                    act.wait_ge(ev["agg2_done"], n["r"])
                    A(AG2[:, :], K1[:, :], ACT.Copy).then_inc(ev["agg2_ready"], 1)
                if mid:
                    act.wait_ge(ev["x1t_done"], n["m"])
                    A(X1H[:, :], K2[:, :], ACT.Copy).then_inc(ev["x1th_ready"], 1)
                    A(X1T[:, :], K2[:, :], ACT.Copy).then_inc(ev["x1t_ready"], 1)
                if rear:
                    act.wait_ge(ev["nat2_done"], n["r"])
                    row_squares(T[:, 16, :], lambda c: cols(K0, c), "ssu_ready", C)
                if mid:
                    act.wait_ge(ev["k_ready"], n["m_prev"])
                    act.wait_ge(ev["q_done"], n["m"])
                    A(QRAW[:, :], K2[:, :], ACT.Copy).then_inc(ev["q_raw"], 1)
                    act.wait_ge(ev["k_done"], n["m"])
                    A(KRAW[:, :], F0[:, :], ACT.Copy).then_inc(ev["k_raw"], 1)
                if rear:
                    act.wait_ge(ev["nu_ready"], n["r"])
                    A(T[:, 19, :], T[:, 18, :], ACT.Tanh).then_inc(ev["tanh_ready"], 1)
                if front:
                    act.wait_ge(ev["agg0_done"], n["f"])
                    A(NMH[:, :], F1[:, :], ACT.Copy).then_inc(ev["nmph_ready"], 1)
                if mid:
                    act.wait_ge(ev["a1_23"], n["m_prev"])
                    sigmoids(0, 2)
                if front:
                    A(NMP[:, :], F1[:, :], ACT.Copy).then_inc(ev["nmp_ready"], 1)
                if mid:
                    sigmoids(2, C)
                if rear:
                    act.wait_ge(ev["x3t_done"], n["r"])
                    A(X3T[:, :], K1[:, :], ACT.Copy).then_inc(ev["x3t_ready"], 1)
                if front:
                    act.wait_ge(ev["xconv_sum"], n["f"])
                    act.wait_ge(ev["gates_done"], n["f_prev"])
                    A(XCH[:, :], XCS[:, :], ACT.Relu, bias=BI[:, 1:2]).then_inc(ev["xch_ready"], 1)
                    A(XC[:, :], XCS[:, :], ACT.Relu, bias=BI[:, 1:2]).then_inc(ev["xconv_ready"], 1)
                if rear:
                    act.wait_ge(ev["agg3_done"], n["r"])
                    A(AG3[:, :], K1[:, :], ACT.Copy).then_inc(ev["agg3_ready"], 1)
                if mid:
                    act.wait_ge(ev["agg1_done"], n["m"])
                    A(AG1[:, :], K2[:, :], ACT.Copy).then_inc(ev["agg1_ready"], 1)
                if front:
                    if not isinstance(t, int) or t + 1 < B:
                        leading_x(n["f_next"], n["f"])
                    act.wait_ge(ev["gater_done"], n["f"])
                    A(R[:, :], F1[:, :], ACT.Sigmoid, bias=BG[:, 0:1]).then_inc(ev["r_ready"], 1)
                    act.wait_ge(ev["gates_done"], n["f"])
                    A(WG[:, :], C0[:, :], ACT.Sigmoid, bias=NBZ[:, :], scale=-1.0).then_inc(ev["w_ready"], 1)

            slots(act, body)

        @block.vector
        def _(dve):
            V = nc.vector
            V.memset(H1H[:, :].bitcast(F32), 0.0)
            V.memset(H1L[:, :].bitcast(F32), 0.0).then_inc(s_set, 1)
            dve.wait_ge(s_const, 64)
            V.tensor_scalar(VE[:, 0:1], PAR[:, V1:V1 + 1], BN_EPS, None, ALU.add)
            V.tensor_scalar(VE[:, 1:2], PAR[:, V2:V2 + 1], BN_EPS, None, ALU.add)
            V.tensor_tensor(BG[:, 0:1], PAR[:, BI_R:BI_R + 1], PAR[:, BH_R:BH_R + 1], ALU.add)
            V.tensor_tensor(BG[:, 1:2], PAR[:, BI_Z:BI_Z + 1], PAR[:, BH_Z:BH_Z + 1], ALU.add).then_inc(s_prep, 1)
            dve.wait_ge(s_prep, 1)
            V.tensor_scalar(NBZ[:, :], BG[:, 1:2], -1.0, None, ALU.mult)
            dve.wait_ge(s_bn_pow, 1)
            V.tensor_tensor(SC[:, 0:1], PAR[:, G1:G1 + 1], RS[:, 0:1], ALU.mult)
            V.tensor_tensor(SC[:, 1:2], PAR[:, G2:G2 + 1], RS[:, 1:2], ALU.mult).then_inc(s_prep, 1)
            dve.wait_ge(s_prep, 2)
            V.tensor_tensor(MS[:, 0:1], PAR[:, M1:M1 + 1], SC[:, 0:1], ALU.mult)
            V.tensor_tensor(MS[:, 1:2], PAR[:, M2:M2 + 1], SC[:, 1:2], ALU.mult).then_inc(s_prep, 1)
            dve.wait_ge(s_prep, 3)
            V.tensor_tensor(BI[:, 0:1], PAR[:, B1:B1 + 1], MS[:, 0:1], ALU.subtract)
            V.tensor_tensor(BI[:, 1:2], PAR[:, B2:B2 + 1], MS[:, 1:2], ALU.subtract).then_inc(s_bn, 1)
            dve.wait_ge(s_weights, 48)
            dve.wait_ge(s_conv2w, 16)
            V.tensor_copy(WH[:, :], W).then_inc(s_prep, 1)
            dve.wait_ge(s_prep, 4)
            V.tensor_tensor(WL[:, :], W, WH[:, :].bitcast(F32), ALU.subtract).then_inc(s_split, 1)

            def norm_stats(layer, src, count):
                L = LT[:, layer, :, :]
                for c in range(C):
                    last = V.bn_stats(ST[:, layer, c, :], src(c))
                last.then_inc(ev["ln_stats"], 1)
                dve.wait_ge(ev["ln_stats"], count)
                even, odd = (lambda k, h=h: ST[:, layer, :, 3 * h + k] for h in (0, 1))
                V.tensor_tensor(L[:, 0, :], even(1), odd(1), ALU.add)
                V.tensor_tensor(L[:, 1, :], even(1), odd(1), ALU.subtract)
                V.tensor_tensor(L[:, 2, :], even(2), odd(2), ALU.add).then_inc(ev["ln_sums"], 1)
                dve.wait_ge(ev["ln_sums"], count)
                V.tensor_scalar(MEAN[:, layer, :], L[:, 0, :], 0.5, None, ALU.mult)
                V.scalar_tensor_tensor(L[:, 3, :], L[:, 1, :], 0.25, L[:, 1, :], ALU.mult, ALU.mult)
                V.tensor_scalar(L[:, 4, :], L[:, 2, :], 1 / P, LN_EPS, ALU.mult, ALU.add).then_inc(
                    ev["ln_parts"], 1)
                dve.wait_ge(ev["ln_parts"], count)
                V.tensor_tensor(VEPS[:, layer, :], L[:, 3, :], L[:, 4, :], ALU.add).then_inc(ev["ln_eps"], 1)

            def norm_apply(layer, src, dst, count, done):
                dve.wait_ge(ev["ln_rstd"], count)
                for c in range(C):
                    last = V.tensor_scalar(dst[:, c, :], src(c), MEAN[:, layer, c:c + 1], RSTD[:, layer, c:c + 1],
                                           ALU.subtract, ALU.mult)
                last.then_inc(ev[done], 1)

            def rest_of_x(count, previous):
                dve.wait_ge(ev["x_loaded"], 16 * count)
                dve.wait_ge(ev["xh"], count)
                dve.wait_ge(ev["x_used"], previous)
                V.tensor_tensor(XL[:, :], X_IN[:, :], XH[:, :].bitcast(F32), ALU.subtract).then_inc(ev["xl"], 1)

            rest_of_x(1, 0)

            def body(t, front, mid, rear, late):
                n = counts(dve, t)
                f, m, r = n["f"], n["m"], n["r"]

                def bias_row(k):
                    return ROWS[:, k, :].unsqueeze(1).to_broadcast([P, C, P])

                def masked0(a, b):
                    for c in range(a, b):
                        dve.wait_ge(ev["exp_ready", c], f)
                        last = V.tensor_tensor(A0[:, c, :], A0[:, c, :], ADJF[:, c, :], ALU.mult)
                    return last

                def masked1(a, b):
                    for c in range(a, b):
                        dve.wait_ge(ev["sig_ready", c], m)
                        last = V.tensor_tensor(A1[:, c, :], SIG[:, c, :], ADJM[:, c, :], ALU.mult)
                    return last

                if rear:
                    dve.wait_ge(ev["dis_ready"], r)
                    dve.wait_ge(ev["dm_ready"], n["r_prev"])
                    V.tensor_copy(DIS_R[:, :], DIS[:, :]).then_inc(ev["dis_kept"], 1)
                if front:
                    dve.wait_ge(ev["h1_ready"], f)
                    dve.wait_ge(ev["conv2_done"], n["f_prev"])
                    V.tensor_tensor(H1L[:, HALF:HALF + N], H1[:, :], H1H[:, HALF:HALF + N].bitcast(F32),
                                    ALU.subtract).then_inc(ev["h1l_ready"], 1)
                if mid:
                    dve.wait_ge(ev["n_ready"], m)
                    V.tensor_tensor(GD[:, :], NG[:, :], XT[:, :], ALU.subtract).then_inc(ev["gate_d"], 1)
                    dve.wait_ge(ev["gate_d"], m)
                    dve.wait_ge(ev["w_ready"], m)
                    V.tensor_tensor(GD[:, :], GD[:, :], WG[:, :], ALU.mult).then_inc(ev["gate_e"], 1)
                    dve.wait_ge(ev["gate_e"], m)
                    V.scalar_tensor_tensor(Y[:, :], XT[:, :], 2.0, GD[:, :], ALU.mult, ALU.add).then_inc(
                        ev["y_ready"], 1)
                if front:
                    dve.wait_ge(ev["msg_done"], f)
                    dve.wait_ge(ev["msg_ready"], n["f_prev"])
                    V.tensor_tensor(MSGA[:, :, :], chunked(F0), bias_row(0), ALU.add).then_inc(ev["msg_added"], 1)
                if late:
                    dve.wait_ge(ev["nat3_done"], n["l"])
                    V.tensor_tensor(RES[:, :, :], chunked(K0), HS[:, :, :], ALU.add).then_inc(ev["res_ready"], 1)
                if front:
                    dve.wait_ge(ev["y_ready"], m)
                    V.tensor_copy(XT[:, :], X_IN[:, :]).then_inc(ev["xcopy"], 1)
                if rear:
                    dve.wait_ge(ev["nrm_pow"], r)
                    V.tensor_scalar(T[:, 2, :], T[:, 1, :], MIN_NORM, None, ALU.max)
                    V.tensor_scalar(T[:, 3, :], T[:, 1, :], MIN_NORM, ATANH_MAX, ALU.max, ALU.min).then_inc(
                        ev["z_ready"], 1)
                    dve.wait_ge(ev["z_ready"], r)
                    V.tensor_scalar(T[:, 4, :], T[:, 3, :], -1.0, 1.0, ALU.mult, ALU.add).then_inc(ev["oneminus"], 1)
                    dve.wait_ge(ev["oneminus"], r)
                    V.reciprocal(T[:, 5, :], T[:, 4, :]).then_inc(ev["rec_ready"], 1)
                    dve.wait_ge(ev["rec_ready"], r)
                    V.scalar_tensor_tensor(T[:, 6, :], T[:, 3, :], 1.0, T[:, 5, :], ALU.add, ALU.mult).then_inc(
                        ev["ratio_ready"], 1)
                    V.reciprocal(T[:, 8, :], T[:, 2, :])
                    V.tensor_scalar(T[:, 14, :], T[:, 3, :], SERIES_BELOW, None, ALU.is_lt)
                    V.tensor_tensor(T[:, 9, :], T[:, 3, :], T[:, 3, :], ALU.mult).then_inc(ev["w_sq"], 1)
                    dve.wait_ge(ev["w_sq"], r)
                if front:
                    dve.wait_ge(ev["zl_ready"], f)
                    dve.wait_ge(ev["zr_ready"], f)
                    V.scalar_tensor_tensor(STL[:, :], F1[:, :], PAR[:, L_A:L_A + 1], ZL[:, :].bitcast(F32),
                                           ALU.mult, ALU.subtract).then_inc(ev["stl_ready"], 1)
                    V.scalar_tensor_tensor(STR[:, :], F1[:, :], PAR[:, R_A:R_A + 1], ZR[:, :].bitcast(F32),
                                           ALU.mult, ALU.subtract).then_inc(ev["str_ready"], 1)
                if rear:
                    V.scalar_tensor_tensor(T[:, 10, :], T[:, 9, :], 7 / 5, T[:, 9, :], ALU.add, ALU.mult).then_inc(
                        ev["ser1"], 1)
                    dve.wait_ge(ev["ser1"], r)
                    V.scalar_tensor_tensor(T[:, 11, :], T[:, 10, :], 7 / 3, T[:, 9, :], ALU.add, ALU.mult).then_inc(
                        ev["ser2"], 1)
                    dve.wait_ge(ev["ser2"], r)
                    V.tensor_scalar(T[:, 13, :], T[:, 11, :], 1 / 7, 1.0, ALU.mult, ALU.add).then_inc(ev["ser3"], 1)
                    dve.wait_ge(ev["ser3"], r)
                if mid:
                    dve.wait_ge(ev["yt_done"], m)
                    norm_stats(0, lambda c: cols(K0, c), n["ln0"])
                if front:
                    dve.wait_ge(ev["adjf_loaded"], 16 * f)
                    dve.wait_ge(ev["agg0_done"], n["f_prev"])
                    masked0(0, 2)
                if rear:
                    dve.wait_ge(ev["ln_ready"], r)
                    V.scalar_tensor_tensor(T[:, 22, :], T[:, 7, :], 0.5, T[:, 8, :], ALU.mult, ALU.mult).then_inc(
                        ev["main_f"], 1)
                    dve.wait_ge(ev["main_f"], r)
                    V.tensor_tensor(T[:, 23, :], T[:, 13, :], T[:, 22, :], ALU.subtract).then_inc(ev["diff_f"], 1)
                    dve.wait_ge(ev["diff_f"], r)
                    V.tensor_tensor(T[:, 24, :], T[:, 23, :], T[:, 14, :], ALU.mult).then_inc(ev["mix_f"], 1)
                    dve.wait_ge(ev["mix_f"], r)
                    V.tensor_tensor(T[:, 25, :], T[:, 22, :], T[:, 24, :], ALU.add).then_inc(ev["f_ready"], 1)
                    dve.wait_ge(ev["f_ready"], r)
                    V.tensor_tensor(XTAN[:, :, :], X2[:, :, :], spread(T[:, 25, :]), ALU.mult).then_inc(
                        ev["xt_ready"], 1)
                if mid:
                    norm_apply(0, lambda c: cols(K0, c), X1, n["ln0"], "x1_ready")
                if front:
                    masked0(2, C).then_inc(ev["a0_ready"], 1)
                if late:
                    dve.wait_ge(ev["res_ready"], n["l"])
                    dve.wait_ge(ev["dm_ready"], n["l"])
                    V.tensor_tensor(RES[:, :, :], RES[:, :, :], spread(DM[:, :]), ALU.mult).then_inc(
                        ev["res_scaled"], 1)
                    dve.wait_ge(ev["res_scaled"], n["l"])
                    V.scalar_tensor_tensor(Z3[:, :, :], RES[:, :, :], 0.0, X3[:, :, :], ALU.max, ALU.add).then_inc(
                        ev["z3_ready"], 1)
                    dve.wait_ge(ev["z3_ready"], n["l"])
                    norm_stats(3, lambda c: Z3[:, c, :], n["ln3"])
                if mid:
                    dve.wait_ge(ev["x1t_ready"], m)
                    V.tensor_tensor(X1L[:, :], X1T[:, :], X1H[:, :].bitcast(F32), ALU.subtract).then_inc(
                        ev["x1tl_ready"], 1)
                if late:
                    dve.wait_ge(ev["out_stored"], 16 * n["l_prev"])
                    norm_apply(3, lambda c: Z3[:, c, :], OUT, n["ln3"], "out_ready")
                if rear:
                    dve.wait_ge(ev["nu_pow"], r)
                    V.tensor_scalar(T[:, 18, :], T[:, 17, :], MIN_NORM, None, ALU.max).then_inc(ev["nu_ready"], 1)
                    dve.wait_ge(ev["nu_ready"], r)
                    V.reciprocal(T[:, 20, :], T[:, 18, :]).then_inc(ev["rnu_ready"], 1)
                if mid:
                    dve.wait_ge(ev["x_done"], m)
                    V.tensor_tensor(XA[:, :, :], chunked(K1), bias_row(1), ALU.add).then_inc(ev["x_added"], 1)
                    dve.wait_ge(ev["q_raw"], m)
                    dve.wait_ge(ev["att_done", C - 1], n["m_prev"])
                    V.scalar_tensor_tensor(QT[:, :], QRAW[:, :], SLOPE, QRAW[:, :], ALU.mult, ALU.max).then_inc(
                        ev["q_ready"], 1)
                    dve.wait_ge(ev["k_raw"], m)
                    V.scalar_tensor_tensor(KT[:, :], KRAW[:, :], SLOPE, KRAW[:, :], ALU.mult, ALU.max).then_inc(
                        ev["k_ready"], 1)
                    dve.wait_ge(ev["x_added"], m)
                    V.scalar_tensor_tensor(XX[:, :, :], XA[:, :, :], SLOPE, XA[:, :, :], ALU.mult,
                                           ALU.max).then_inc(ev["xact_ready"], 1)
                if rear:
                    dve.wait_ge(ev["rnu_ready"], r)
                    dve.wait_ge(ev["tanh_ready"], r)
                    V.tensor_tensor(T[:, 21, :], T[:, 19, :], T[:, 20, :], ALU.mult).then_inc(ev["g_ready"], 1)
                    dve.wait_ge(ev["g_ready"], r)
                    V.tensor_tensor(T[:, 26, :], T[:, 21, :], T[:, 17, :], ALU.mult).then_inc(ev["ny_ready"], 1)
                    dve.wait_ge(ev["ny_ready"], r)
                    V.tensor_scalar(T[:, 27, :], T[:, 26, :], MIN_NORM, None, ALU.max).then_inc(ev["nyc_ready"], 1)
                    dve.wait_ge(ev["nyc_ready"], r)
                    V.reciprocal(T[:, 28, :], T[:, 27, :]).then_inc(ev["rny_ready"], 1)
                    dve.wait_ge(ev["rny_ready"], r)
                    V.tensor_scalar(T[:, 29, :], T[:, 28, :], BALL, 1.0, ALU.mult, ALU.min).then_inc(
                        ev["fac_ready"], 1)
                    dve.wait_ge(ev["fac_ready"], r)
                    V.tensor_tensor(T[:, 30, :], T[:, 21, :], T[:, 29, :], ALU.mult).then_inc(ev["g2_ready"], 1)
                    dve.wait_ge(ev["g2_ready"], r)
                    for c in range(C):
                        last = V.scalar_tensor_tensor(Z2[:, c, :], cols(K0, c), T[:, 30, c:c + 1], X2[:, c, :],
                                                      ALU.mult, ALU.add)
                    last.then_inc(ev["z2_ready"], 1)
                    dve.wait_ge(ev["z2_ready"], r)
                    norm_stats(2, lambda c: Z2[:, c, :], n["ln2"])
                if mid:
                    dve.wait_ge(ev["adjm_loaded"], 16 * m)
                    dve.wait_ge(ev["agg1_done"], n["m_prev"])
                    masked1(0, 2).then_inc(ev["a1_01"], 1)
                if rear:
                    norm_apply(2, lambda c: Z2[:, c, :], X3, n["ln2"], "x3_ready")
                if mid:
                    masked1(2, C).then_inc(ev["a1_23"], 1)
                    dve.wait_ge(ev["a1_23"], m)
                    dve.wait_ge(ev["deg_done"], n["m_prev"])
                    V.tensor_tensor(ASUM[:, 1, :], A1[:, 2, :], A1[:, 3, :], ALU.add).then_inc(ev["asum23"], 1)
                    dve.wait_ge(ev["asum23"], m)
                    dve.wait_ge(ev["asum01"], m)
                    V.tensor_tensor(ASUM[:, 2, :], ASUM[:, 0, :], ASUM[:, 1, :], ALU.add).then_inc(
                        ev["asum_ready"], 1)
                if front:
                    dve.wait_ge(ev["nmp_ready"], f)
                    V.tensor_tensor(NML[:, :], NMP[:, :], NMH[:, :].bitcast(F32), ALU.subtract).then_inc(
                        ev["nmpl_ready"], 1)
                if rear:
                    dve.wait_ge(ev["hlin_done"], r)
                    V.tensor_tensor(HL[:, :, :], chunked(K2), bias_row(2), ALU.add).then_inc(ev["hlin_added"], 1)
                    dve.wait_ge(ev["hlin_added"], r)
                    V.tensor_tensor(HS[:, :, :], HL[:, :, :], spread(DIS_R[:, :]), ALU.mult).then_inc(
                        ev["hs_ready"], 1)
                if mid:
                    dve.wait_ge(ev["deg_done"], m)
                    V.tensor_copy(D[:, 0, :], K0[:, 0:C])
                    V.tensor_scalar(D[:, 5, :], K0[:, C:2 * C], 1.0, DEG_EPS, ALU.add, ALU.add).then_inc(
                        ev["dis_eps"], 1)
                    dve.wait_ge(ev["dis_eps"], m)
                    V.tensor_scalar(D[:, 1, :], D[:, 0, :], 0.0, None, ALU.is_equal).then_inc(ev["d_zero"], 1)
                    dve.wait_ge(ev["d_zero"], m)
                    V.tensor_tensor(D[:, 2, :], D[:, 0, :], D[:, 1, :], ALU.add).then_inc(ev["d_safe"], 1)
                    dve.wait_ge(ev["d_safe"], m)
                    V.tensor_scalar(D[:, 4, :], D[:, 1, :], -1.0, 1.0, ALU.mult, ALU.add).then_inc(ev["d_mask"], 1)
                    dve.wait_ge(ev["d_mask"], m)
                if front:
                    dve.wait_ge(ev["conv2_done"], f)
                    V.scalar_tensor_tensor(XCS[:, :], CONV[:, :], SC[:, 1:2], XT[:, :], ALU.mult, ALU.add).then_inc(
                        ev["xconv_sum"], 1)
                if mid:
                    dve.wait_ge(ev["d_pow"], m)
                    V.tensor_tensor(DINV[:, :], D[:, 3, :], D[:, 4, :], ALU.mult).then_inc(ev["dinv_ready"], 1)
                    dve.wait_ge(ev["dinv_ready"], m)
                    dve.wait_ge(ev["xact_ready"], m)
                    V.tensor_tensor(XS[:, :, :], XX[:, :, :], spread(DINV[:, :]), ALU.mult).then_inc(
                        ev["xs_ready"], 1)
                if front:
                    dve.wait_ge(ev["xconv_ready"], f)
                    V.tensor_tensor(XCL[:, :], XC[:, :], XCH[:, :].bitcast(F32), ALU.subtract).then_inc(
                        ev["xcl_ready"], 1)
                if mid:
                    dve.wait_ge(ev["nat1_done"], m)
                    for c in range(C):
                        last = V.scalar_tensor_tensor(Z1[:, c, :], cols(K1, c), DINV[:, c:c + 1], X1[:, c, :],
                                                      ALU.mult, ALU.add)
                    last.then_inc(ev["z1_ready"], 1)
                    dve.wait_ge(ev["z1_ready"], m)
                    norm_stats(1, lambda c: Z1[:, c, :], n["ln1"])
                more = not isinstance(t, int) or t + 1 < B
                if front:
                    if more:
                        rest_of_x(n["f_next"], f)
                    dve.wait_ge(ev["r_ready"], f)
                    V.scalar_tensor_tensor(GT[:, :], F0[:, :], PAR[:, BH_N:BH_N + 1], R[:, :], ALU.add,
                                ALU.mult).then_inc(ev["gate_t"], 1)
                    dve.wait_ge(ev["gate_t"], f)
                if mid:
                    norm_apply(1, lambda c: Z1[:, c, :], X2, n["ln1"], "x2_ready")
                if front:
                    dve.wait_ge(ev["gates_done"], f)
                    V.tensor_tensor(GT[:, :], GT[:, :], C1[:, :], ALU.add).then_inc(ev["gate_u"], 1)
                if rear:
                    dve.wait_ge(ev["mask_loaded"], 16 * r)
                    V.tensor_tensor(DM[:, :], DIS_R[:, :], MASK[:, :], ALU.mult).then_inc(ev["dm_ready"], 1)

            slots(dve, body)

        @block.tensor
        def _(pe):
            mm = nc.tensor.matmul

            def product(out, terms):
                k = 0
                for wgt, mov in terms:
                    for i, j in ((0, 0), (0, 1), (1, 0)):
                        last = mm(out, wgt[i], mov[j], start=(k == 0), stop=(k == 3 * len(terms) - 1))
                        k += 1
                return last

            def weight(at_col):
                return WH[:, at_col:at_col + P], WL[:, at_col:at_col + P]

            def transposed(out, tile):
                for c in range(C):
                    last = nc.tensor.transpose(cols(out, c), tile(c), IDENT[:, :])
                return last

            def aggregate(out, rows, chunks):
                for c in range(C):
                    last = mm(out[:, :], rows[:, c, :], chunks[:, c, :], start=(c == 0), stop=(c == C - 1))
                return last

            pe.wait_ge(s_const, 64)
            pe.wait_ge(s_split, 1)
            pe.wait_ge(s_set, 4)
            pe.wait_ge(s_weights, 48)

            def body(t, front, mid, rear, late):
                n = counts(pe, t)
                f, m, r = n["f"], n["m"], n["r"]
                xt = (XH[:, :], XL[:, :])
                x1t = (X1H[:, :], X1L[:, :])

                def taps(a, b):
                    for k in range(a, b):
                        for i, (w, h) in enumerate(((WH, H1H), (WH, H1L), (WL, H1H))):
                            last = mm(CONV[:, :], w[:, W_CONV2 + k * P:W_CONV2 + (k + 1) * P], h[:, k:k + N],
                                      start=(k == 0 and i == 0), stop=(k == TAPS - 1 and i == 2))
                    return last

                def distances(c):
                    mm(CB[c % 2][:, :], cols(STL, c), STR[:, :], start=True, stop=True).then_inc(
                        ev["dist_done", c], 1)

                if front:
                    pe.wait_ge(ev["xl"], f)
                    pe.wait_ge(ev["r_ready"], n["f_prev"])
                    product(F1[:, :], [(weight(W_SE), xt)]).then_inc(ev["g1_done"], 1)
                    pe.wait_ge(ev["gate_t"], n["f_prev"])
                    product(F0[:, :], [(weight(W_CONV1), xt)]).then_inc(ev["conv1_done"], 1)
                    pe.wait_ge(ev["sq_ready"], f)
                    mm(F1[:, :], SQMAT[:, :], SQ[:, :], start=False, stop=True, skip_group_check=True).then_inc(
                        ev["g_done"], 1)
                    pe.wait_ge(ev["h1_ready"], f)
                    for c in range(C):
                        last = product(cols(F0, c), [((cols(XH, c), cols(XL, c)), weight(W_MSG))])
                    last.then_inc(ev["msg_done"], 1)
                    pe.wait_ge(ev["h1l_ready"], f)
                    pe.wait_ge(ev["xconv_sum"], n["f_prev"])
                    taps(0, 3)
                if mid:
                    pe.wait_ge(ev["y_ready"], m)
                    pe.wait_ge(ev["res_ready"], n["r_prev"])
                    transposed(K0, lambda c: cols(Y, c)).then_inc(ev["yt_done"], 1)
                if front:
                    pe.wait_ge(ev["stl_ready"], f)
                    pe.wait_ge(ev["str_ready"], f)
                    pe.wait_ge(ev["w_ready"], n["f_prev"])
                    distances(0)
                    pe.wait_ge(ev["gate_u"], n["f_prev"])
                    distances(1)
                    taps(3, 5)
                    pe.wait_ge(ev["exp_ready", 0], f)
                    distances(2)
                    taps(5, 6)
                    pe.wait_ge(ev["exp_ready", 1], f)
                    distances(3)
                    taps(6, 8)
                if rear:
                    pe.wait_ge(ev["xt_ready"], r)
                    pe.wait_ge(ev["adjr_loaded"], 16 * r)
                    pe.wait_ge(ev["z1_ready"], n["m_prev"])
                    aggregate(K1, XTAN, ADJR).then_inc(ev["agg2_done"], 1)
                if mid:
                    pe.wait_ge(ev["x1_ready"], m)
                    pe.wait_ge(ev["agg1_ready"], n["m_prev"])
                    transposed(K2, lambda c: X1[:, c, :]).then_inc(ev["x1t_done"], 1)
                if front:
                    taps(8, 9)
                if rear:
                    pe.wait_ge(ev["agg2_ready"], r)
                    pe.wait_ge(ev["x1_ready"], m)
                    transposed(K0, lambda c: cols(AG2, c)).then_inc(ev["nat2_done"], 1)
                if front:
                    taps(9, 10)
                if mid:
                    pe.wait_ge(ev["x1tl_ready"], m)
                    pe.wait_ge(ev["x1th_ready"], m)
                    pe.wait_ge(ev["x1t_ready"], m)
                    product(K2[:, :], [(weight(W_Q), x1t)]).then_inc(ev["q_done"], 1)
                    pe.wait_ge(ev["msg_added"], f)
                    product(F0[:, :], [(weight(W_K), x1t)]).then_inc(ev["k_done"], 1)
                    pe.wait_ge(ev["agg2_ready"], r)
                    for c in range(C):
                        last = product(cols(K1, c), [((cols(X1H, c), cols(X1L, c)), weight(W_LIN))])
                    last.then_inc(ev["x_done"], 1)
                if front:
                    pe.wait_ge(ev["msg_ready"], f)
                    pe.wait_ge(ev["a0_ready"], f)
                    aggregate(F1, MSG, A0).then_inc(ev["agg0_done"], 1)
                if mid:
                    pe.wait_ge(ev["q_ready"], m)
                    pe.wait_ge(ev["k_ready"], m)
                    for c in range(C):
                        if c < 2:
                            pe.wait_ge(ev["exp_ready", c + 2], f)
                        else:
                            pe.wait_ge(ev["sig_ready", c - 2], m)
                        mm(CB[c % 2][:, :], cols(KT, c), QT[:, :], start=True, stop=True).then_inc(
                            ev["att_done", c], 1)
                if front:
                    taps(10, 13)
                if rear:
                    pe.wait_ge(ev["x3_ready"], r)
                    pe.wait_ge(ev["x_added"], m)
                    transposed(K1, lambda c: X3[:, c, :]).then_inc(ev["x3t_done"], 1)
                if front:
                    taps(13, 14)
                if rear:
                    pe.wait_ge(ev["x3t_ready"], r)
                    pe.wait_ge(ev["q_raw"], m)
                    for c in range(C):
                        last = mm(cols(K2, c), cols(X3T, c), WOUT[:, :], start=True, stop=True)
                    last.then_inc(ev["hlin_done"], 1)
                if front:
                    taps(14, 15)
                if mid:
                    pe.wait_ge(ev["asum_ready"], m)
                    pe.wait_ge(ev["dsum_ready"], m)
                    pe.wait_ge(ev["z2_ready"], r)
                    for c in range(C):
                        mm(K0[:, c:c + 1], cols(ASUM[:, 2, :], c), ONES[:, :], start=True, stop=True)
                    for c in range(C):
                        last = mm(K0[:, C + c:C + c + 1], cols(DSUM[:, 2, :], c), ONES[:, :], start=True, stop=True)
                    last.then_inc(ev["deg_done"], 1)
                if front:
                    taps(15, TAPS).then_inc(ev["conv2_done"], 1)
                if rear:
                    pe.wait_ge(ev["hs_ready"], r)
                    aggregate(K1, HS, ADJR).then_inc(ev["agg3_done"], 1)
                if mid:
                    pe.wait_ge(ev["xs_ready"], m)
                    pe.wait_ge(ev["hlin_added"], r)
                    aggregate(K2, XS, A1).then_inc(ev["agg1_done"], 1)
                if rear:
                    pe.wait_ge(ev["agg3_ready"], r)
                    pe.wait_ge(ev["dis_eps"], m)
                    transposed(K0, lambda c: cols(AG3, c)).then_inc(ev["nat3_done"], 1)
                if front:
                    xc, nm = (XCH[:, :], XCL[:, :]), (NMH[:, :], NML[:, :])

                    def gate(bank, first, last, terms):
                        k = 0
                        for wgt, mov in terms:
                            for i, j in ((0, 0), (0, 1), (1, 0)):
                                k += 1
                                done = mm(bank[:, :], wgt[i], mov[j], start=(first and k == 1),
                                          stop=(last and k == 3 * len(terms)))
                        return done

                    pe.wait_ge(ev["nmpl_ready"], f)
                    pe.wait_ge(ev["nmph_ready"], f)
                    pe.wait_ge(ev["nmp_ready"], f)
                    pe.wait_ge(ev["k_raw"], m)
                    pe.wait_ge(ev["sig_ready", 2], m)
                    pe.wait_ge(ev["sig_ready", 3], m)
                    gate(F0, True, True, [(weight(W_HH + 2 * P), xt)])
                    gate(F1, True, False, [(weight(W_HH), xt)])
                    gate(C0, True, False, [(weight(W_HH + P), xt)]).then_inc(ev["x_used"], 1)
                if mid:
                    pe.wait_ge(ev["agg1_ready"], m)
                    pe.wait_ge(ev["agg3_ready"], r)
                    transposed(K1, lambda c: cols(AG1, c)).then_inc(ev["nat1_done"], 1)
                if front:
                    pe.wait_ge(ev["xcl_ready"], f)
                    gate(F1, False, True, [(weight(W_IH + 3 * P), nm), (weight(W_IH), xc)]).then_inc(
                        ev["gater_done"], 1)
                    gate(C0, False, True, [(weight(W_IH + 4 * P), nm), (weight(W_IH + P), xc)])
                    gate(C1, True, True, [(weight(W_IH + 5 * P), nm), (weight(W_IH + 2 * P), xc)]).then_inc(
                        ev["gates_done"], 1)

            slots(pe, body)


def packed(i):
    t = lambda a: np.asarray(a).T
    zeros = np.zeros
    w_se = zeros((P, P), np.float32)
    for g in range(3):
        w_se[:, 5 * g:5 * g + 3] = t(i["L0_gnn_w_se"])
    conv2 = np.asarray(i["L0_gnn_conv2_w"]).transpose(1, 2, 0).reshape(P, TAPS * P)
    w_ih = np.asarray(i["L0_gnn_w_ih"])
    weights = np.concatenate(
        [t(i["L0_gnn_conv1_w"][:, :, 0]), conv2, w_se, t(i["L0_gnn_w_msg"]), i["L1_gnn_W_lin"], i["L1_gnn_W_q"],
         i["L1_gnn_W_k"], t(w_ih[:, :P]), t(w_ih[:, P:]), t(i["L0_gnn_w_hh"]), t(i["L3_gnn_W"])], axis=1)
    rows = np.broadcast_to(np.stack([i["L0_gnn_b_msg"], i["L1_gnn_b_lin"], i["L3_gnn_b"]]), (P, 3, P))
    par = zeros((P, N_PAR), np.float32)
    for k, name in enumerate(("bn1_g", "bn1_b", "bn1_m", "bn1_v", "bn2_g", "bn2_b", "bn2_m", "bn2_v")):
        par[:, k] = i["L0_gnn_" + name]
    for k, name in ((BI_R, "b_ih"), (BH_R, "b_hh")):
        par[:, k:k + 3] = t(np.asarray(i["L0_gnn_" + name]).reshape(3, P))
    sqmat = zeros((P, P), np.float32)
    par[0:3, SQ_BIAS] = i["L0_gnn_b_se"]
    par[3, SQ_BIAS] = 1
    left, right = (1, 1, 1, 0, 1), (2, 2, 2, 1, 0)
    for g in range(3):
        s = slice(5 * g, 5 * g + 5)
        par[s, L_A], par[s, R_A] = left, right
        for rest, a, za, zc, one in ((g == 1, left, L_ZA, L_ZC, 3), (g == 2, right, R_ZA, R_ZC, 4)):
            if rest:
                par[s, za] = a
            else:
                par[5 * g + one, zc] = -1
        sqmat[3, 5 * g:5 * g + 3] = i["L0_gnn_b_se"]
        sqmat[0:3, 5 * g + 3:5 * g + 5] = -1
    c = np.ascontiguousarray
    return {
        "xT": c(np.asarray(i["x"]).transpose(0, 2, 1)), "adjT": c(np.asarray(i["adj"]).transpose(0, 2, 1)),
        "mask": c(np.asarray(i["nodemask"]).reshape(B, C, P).transpose(0, 2, 1)), "weights": c(weights),
        "rows": c(rows), "params": par, "sqmat": sqmat, "ident": np.eye(P, dtype=np.float32),
    }


def kernel(**inputs):
    import concourse.bacc as bacc
    from concourse.bass_utils import run_bass_kernel_spmd

    arrays = packed(inputs)
    nc = bacc.Bacc("TRN2", target_bir_lowering=False, num_devices=1)
    args = [nc.dram_tensor("in_" + k, a.shape, mybir.dt.from_np(a.dtype), kind="ExternalInput").ap()
            for k, a in arrays.items()]
    out = nc.dram_tensor("out", (B, N, P), F32, kind="ExternalOutput").ap()
    adj_resnorm_kernel(nc, *args, out)
    got = run_bass_kernel_spmd(nc, [{"in_" + k: a for k, a in arrays.items()}], core_ids=[0])
    return got.results[0]["out"]
```

```python
from contextlib import ExitStack

import numpy as np
import concourse.bass as bass
from concourse import mybir

F32 = mybir.dt.float32
F32R = mybir.dt.float32r
ALU = mybir.AluOpType
ACT = mybir.ActivationFunctionType

P = 128
B, N = 16, 512
C = N // P
TAPS = 17
HALF = TAPS // 2
PADDED = N + 2 * HALF
LN_EPS = 1e-5
BN_EPS = 1e-5
DEG_EPS = 1e-8
MIN_NORM = 1e-15
SLOPE = 0.01
BALL = 0.996
ATANH_MAX = 1 - 1e-7
SERIES_BELOW = 0.1

W_CONV1, W_SE, W_MSG, W_CONV2 = 0, P, 2 * P, 3 * P
W_LIN = W_CONV2 + TAPS * P
W_Q, W_K = W_LIN + P, W_LIN + 2 * P
W_IH = W_LIN + 3 * P
W_HH = W_IH + 6 * P
W_SPLIT = W_HH + 3 * P

(G1, B1, M1, V1, G2, B2, M2, V2, BI_R, BI_Z, BI_N, BH_R, BH_Z, BH_N,
 SQ_BIAS, L_A, L_ZA, L_ZC, R_A, R_ZA, R_ZC) = range(21)
N_PAR = 21

EVENTS = (
    "dist_done exp_ready att_done sig_ready "
    "xh xl xcopy sq_ready zr_ready str_ready h1_ready h1l_ready "
    "msg_added msh_ready msl_ready xconv_sum xconv_ready xcl_ready nmph_ready nmpl_ready "
    "gatez_done r_ready w_ready gate_t gate_u n_ready gate_d gate_e y_ready x_used gater_done "
    "a0_01 a0_23 a0h_01 a0h_23 a0l_01 a0l_23 a1_01 a1_23 "
    "g1_done conv1_done msg_done g_done conv2_done agg0_done gates_done yt_done "
    "ln_stats ln_sums ln_parts ln_eps ln_rstd ln_shift x1_ready "
    "x1t_done x1th_ready x1tl_ready x_done q_done k_done q_raw k_raw q_ready k_ready x_added xact_ready "
    "asum01 asum23 asum_ready dsum23 adjh_01 adjh_23 adjl_ready dsum_ready deg_done "
    "d_zero d_safe d_pow d_mask dinv_ready "
    "dis_eps dis_ready xs_ready agg1_done agg1_ready nat1_done z1_ready "
    "dis_kept var_ready x2_ready nrm_ready z_ready oneminus rec_ready ratio_ready ln_ready "
    "w_sq ser1 ser2 ser3 main_f diff_f mix_f f_ready xth_ready xt_ready agg2_done agg2_ready nat2_done "
    "ssu_ready nu_pow nu_ready tanh_ready rnu_ready g_ready ny_ready nyc_ready rny_ready fac_ready g2_ready z2_ready "
    "x3_ready x3t_done x3t_ready hlin_done hlin_added hs_ready hsh_ready hsl_ready "
    "agg3_done agg3_ready nat3_done dm_ready res_ready res_scaled z3_ready out_ready"
).split()
DMA_EVENTS = "x_loaded adjf_loaded adjm_loaded mask_loaded out_stored".split()


def adj_resnorm_kernel(nc, xT_d, adjT_d, mask_d, weights_d, rows_d, params_d, sqmat_d, ident_d, out_d):
    ctx = ExitStack()
    with ctx:
        def sb(name, shape, dt=F32):
            return ctx.enter_context(nc.sbuf_tensor(name, shape, dt))

        def bank(name):
            return ctx.enter_context(nc.psum_tensor(name, [P, N], F32))

        def sem(name):
            return ctx.enter_context(nc.semaphore(name))

        WOUT = sb("WOUT", [P, P])
        WH = sb("WH", [P, W_SPLIT], F32R)
        WL = sb("WL", [P, W_SPLIT], F32R)
        ROWS = sb("ROWS", [P, 3, P])
        PAR = sb("PAR", [P, N_PAR])
        SQMAT = sb("SQMAT", [P, P])
        IDENT = sb("IDENT", [P, P])
        ONES = sb("ONES", [P, 1])
        POW = sb("POW", [P, 2, C])
        VE = sb("VE", [P, 2])
        RS = sb("RS", [P, 2])
        SC = sb("SC", [P, 2])
        MS = sb("MS", [P, 2])
        BI = sb("BI", [P, 2])
        BG = sb("BG", [P, 2])
        NBZ = sb("NBZ", [P, 1])

        X_IN = sb("X_IN", [P, N])
        ADJF = sb("ADJF", [P, C, N])
        ADJM = sb("ADJM", [P, C, N])
        ADJH = sb("ADJH", [P, C, N], F32R)
        ADJL = sb("ADJL", [P, C, N], F32R)
        MASK = sb("MASK", [P, C])

        XT, XH, XL = sb("XT", [P, N]), sb("XH", [P, N], F32R), sb("XL", [P, N], F32R)
        SQ = sb("SQ", [P, N])
        A0L = sb("A0L", [P, C, N], F32R)
        ZL, ZR, STL, STR = (A0L[:, k, :] for k in range(4))
        H1 = sb("H1", [P, N])
        H1H, H1L = sb("H1H", [P, PADDED], F32R), sb("H1L", [P, PADDED], F32R)
        XC = sb("XC", [P, N])
        XCH, XCL = sb("XCH", [P, N], F32R), sb("XCL", [P, N], F32R)
        MSG = sb("MSG", [P, C, P])
        MSH, MSL = sb("MSH", [P, C, P], F32R), sb("MSL", [P, C, P], F32R)
        A0 = sb("A0", [P, C, N])
        A0H = sb("A0H", [P, C, N], F32R)
        NMH, NML = sb("NMH", [P, N], F32R), sb("NML", [P, N], F32R)
        R, WG, NG = sb("R", [P, N]), sb("WG", [P, N]), sb("NG", [P, N])
        GT, Y = sb("GT", [P, N]), sb("Y", [P, N])
        X1 = sb("X1", [P, C, P])

        X1H, X1L = sb("X1H", [P, N], F32R), sb("X1L", [P, N], F32R)
        XX, XS = sb("XX", [P, C, P]), sb("XS", [P, C, P])
        QRAW, KRAW, QT, KT = (sb(n, [P, N]) for n in ("QRAW", "KRAW", "QT", "KT"))
        BIG = sb("BIG", [P, 2, C, N])
        SIG, A1 = BIG[:, 0, :, :], BIG[:, 1, :, :]
        W = BIG[:, :, :, :].rearrange("p a c n -> p (a c n)")
        ASUM = sb("ASUM", [P, 3, N])
        DSUM = sb("DSUM", [P, 3, N])
        D = sb("D", [P, 8, C])
        DINV, DIS, DIS_R = sb("DINV", [P, C]), sb("DIS", [P, C]), sb("DIS_R", [P, C])
        Z1, X2 = sb("Z1", [P, C, P]), sb("X2", [P, C, P])

        JUNK = sb("JUNK", [P, C, P], mybir.dt.bfloat16)
        T = sb("T", [P, 32, C])
        FH, FL = sb("FH", [P, C, P], F32R), sb("FL", [P, C, P], F32R)
        AG = sb("AG", [P, N])
        Z2, X3 = sb("Z2", [P, C, P]), sb("X3", [P, C, P])
        X3T, HS = sb("X3T", [P, N]), sb("HS", [P, C, P])
        RES, Z3 = sb("RES", [P, C, P]), sb("Z3", [P, C, P])
        DM = sb("DM", [P, C])
        OUT = sb("OUT", [P, C, P])

        ROW = (0, 3, 1, 2)
        ST = sb("ST", [P, 4, C, 6])
        LT = sb("LT", [P, 4, 5, C])
        NMEAN = sb("NMEAN", [P, 4, C])
        SHIFT = sb("SHIFT", [P, 4, C])
        VEPS = sb("VEPS", [P, 5, C])
        RSTD = sb("RSTD", [P, 5, C])

        CONV, F0, F1, C0, C1, K0, K1, K2 = (bank(n) for n in ("CONV", "F0", "F1", "C0", "C1", "K0", "K1", "K2"))
        CB = (C0, C1)

        ev = {n: sem("s_" + n) for n in EVENTS + DMA_EVENTS}
        s_const, s_leading, s_split, s_prep = (sem(n) for n in ("s_const", "s_leading", "s_split", "s_prep"))
        s_first_w, s_conv2_w, s_rest_w = sem("s_first_w"), sem("s_conv2_w"), sem("s_rest_w")
        s_set, s_bn_pow, s_bn = sem("s_set"), sem("s_bn_pow"), sem("s_bn")

        def at(e, t, k):
            return max(0, min(t + k, B)) if isinstance(t, int) else (e.snap(t + k) if k else t)

        def counts(e, t):
            n = {k: at(e, t, k) for k in (2, 1, 0, -1, -2)}
            n = {"f_next": n[2], "f": n[1], "f_prev": n[0], "m": n[0], "m_prev": n[-1], "r": n[-1],
                 "r_prev": n[-2]}
            if e is not nc.sync and e is not nc.tensor:
                if isinstance(t, int):
                    n["ln0"] = n["m"] + n["m_prev"] + 2 * n["r_prev"]
                    n["ln2"] = n["m"] + n["m_prev"] + n["r"] + n["r_prev"]
                    n["ln3"] = n["m"] + n["m_prev"] + 2 * n["r"]
                    n["ln1"] = 2 * n["m"] + 2 * n["r"]
                    n["ln1_prev"] = 2 * n["m_prev"] + 2 * n["r_prev"]
                    n["ln3_prev"] = n["m_prev"] + at(e, t, -2) + 2 * n["r_prev"]
                else:
                    for k, name in ((5, "ln0"), (4, "ln2"), (3, "ln3"), (2, "ln1"), (6, "ln1_prev"), (7, "ln3_prev")):
                        n[name] = e.snap(4 * t - k)
            return n

        def nth(chunk, graphs):
            n = C * graphs - (C - 1 - chunk)
            return max(0, n) if isinstance(n, int) else n

        def slots(e, body):
            for t in range(4):
                body(t, True, t >= 1, t >= 2)
            with e.Fori(4, B - 1) as t:
                body(t, True, True, True)
            body(B - 1, True, True, True)
            body(B, False, True, True)
            body(B + 1, False, False, True)

        def spread(v):
            return v.unsqueeze(2).to_broadcast([P, C, P])

        def chunked(t):
            return t[:, :].rearrange("p (c n) -> p c n", c=C)

        def cols(t, c):
            return t[:, c * P:(c + 1) * P]

        block = ctx.enter_context(nc.Block())

        @block.sync
        def _(sp):
            sp.dma_start(X_IN[:, :], xT_d[0]).then_inc(ev["x_loaded"], 16)
            sp.dma_start(W[:, 0:W_CONV2], weights_d[:, 0:W_CONV2]).then_inc(s_first_w, 16)
            sp.dma_start(PAR[:, :], params_d).then_inc(s_const, 16)
            sp.dma_start(SQMAT[:, :], sqmat_d).then_inc(s_const, 16)
            sp.dma_start(IDENT[:, :], ident_d).then_inc(s_const, 16)
            sp.dma_start(ROWS[:, :, :], rows_d).then_inc(s_const, 16)
            sp.dma_start(W[:, W_CONV2:W_LIN], weights_d[:, W_CONV2:W_LIN]).then_inc(s_conv2_w, 16)
            sp.dma_start(ADJF[:, :, :], adjT_d[0].rearrange("(c p) n -> p c n", p=P)).then_inc(ev["adjf_loaded"], 16)
            sp.dma_start(W[:, W_LIN:], weights_d[:, W_LIN:W_SPLIT]).then_inc(s_rest_w, 16)
            sp.dma_start(WOUT[:, :], weights_d[:, W_SPLIT:]).then_inc(s_rest_w, 16)

            def store(graph, count):
                sp.wait_ge(ev["out_ready"], count)
                sp.dma_start(out_d[graph].rearrange("(c p) d -> p c d", p=P), OUT[:, :, :]).then_inc(
                    ev["out_stored"], 16)

            def loads(t, front, mid, rear):
                n = counts(sp, t)
                static = isinstance(t, int)
                if not static or t + 1 < B:
                    nxt = sp.snap(t + 1) if not static else t + 1
                    sp.wait_ge(ev["xh"], n["f"])
                    sp.wait_ge(ev["xl"], n["f"])
                    sp.wait_ge(ev["xcopy"], n["f"])
                    sp.dma_start(X_IN[:, :], xT_d[nxt]).then_inc(ev["x_loaded"], 16)
                    sp.wait_ge(ev["a0_01"], n["f"])
                    sp.wait_ge(ev["a0_23"], n["f"])
                    sp.dma_start(ADJF[:, :, :], adjT_d[nxt].rearrange("(c p) n -> p c n", p=P)).then_inc(
                        ev["adjf_loaded"], 16)
                if not static or t < B:
                    sp.wait_ge(ev["a1_23"], n["m"])
                    sp.wait_ge(ev["dsum23"], n["m"])
                    sp.wait_ge(ev["adjl_ready"], n["m"])
                    sp.dma_start(ADJM[:, :, :], adjT_d[t].rearrange("(c p) n -> p c n", p=P)).then_inc(
                        ev["adjm_loaded"], 16)
                if not static or 0 <= t - 1 < B:
                    last = sp.snap(t - 1) if not static else t - 1
                    sp.wait_ge(ev["dm_ready"], n["r"])
                    sp.dma_start(MASK[:, :], mask_d[last]).then_inc(ev["mask_loaded"], 16)
                if not static or t >= 3:
                    store(sp.snap(t - 3) if not static else t - 3, n["r_prev"])

            slots(sp, loads)
            store(B - 1, B)
            sp.wait_ge(ev["out_stored"], 16 * B)

        @block.gpsimd
        def _(pool):
            nc.gpsimd.memset(POW[:, 0, :], -0.5).then_inc(s_set, 1)
            nc.gpsimd.memset(POW[:, 1, :], 0.5).then_inc(s_set, 1)
            nc.gpsimd.memset(ONES[:, :], 1.0).then_inc(s_set, 1)
            pool.wait_ge(s_set, 3)
            pool.wait_ge(s_prep, 1)
            nc.gpsimd.tensor_tensor(RS[:, :], VE[:, :], POW[:, 0, 0:2], ALU.pow).then_inc(s_bn_pow, 1)

            def rstd(layer, count):
                pool.wait_ge(ev["ln_eps"], count)
                row = ROW[layer]
                nc.gpsimd.tensor_tensor(RSTD[:, row, :], VEPS[:, row, :], POW[:, 0, :], ALU.pow).then_inc(
                    ev["ln_rstd"], 1)
                shift(layer, row, count)

            def rest_of_h1(count, previous):
                pool.wait_ge(ev["h1_ready"], count)
                pool.wait_ge(ev["conv2_done"], previous)
                nc.gpsimd.tensor_tensor(H1L[:, HALF:HALF + N], H1[:, :], H1H[:, HALF:HALF + N].bitcast(F32),
                                ALU.subtract).then_inc(ev["h1l_ready"], 1)

            def shift(layer, row, count):
                pool.wait_ge(ev["ln_rstd"], count)
                nc.gpsimd.tensor_tensor(SHIFT[:, layer, :], NMEAN[:, layer, :], RSTD[:, row, :], ALU.mult).then_inc(
                    ev["ln_shift"], 1)

            def body(t, front, mid, rear):
                n = counts(pool, t)
                if mid:
                    rstd(0, n["ln0"])
                if front:
                    pool.wait_ge(ev["adjf_loaded"], 16 * n["f"])
                    pool.wait_ge(ev["agg0_done"], n["f_prev"])
                    for c in range(C // 2, C):
                        pool.wait_ge(ev["exp_ready"], nth(c, n["f"]))
                        last = nc.gpsimd.tensor_tensor(A0[:, c, :], A0[:, c, :], ADJF[:, c, :], ALU.mult)
                    last.then_inc(ev["a0_23"], 1)
                if mid:
                    pool.wait_ge(ev["adjm_loaded"], 16 * n["m"])
                    pool.wait_ge(ev["deg_done"], n["m_prev"])
                    nc.gpsimd.tensor_tensor(DSUM[:, 0, :], ADJM[:, 0, :], ADJM[:, 1, :], ALU.add)
                    nc.gpsimd.tensor_tensor(DSUM[:, 1, :], ADJM[:, 2, :], ADJM[:, 3, :], ALU.add).then_inc(
                        ev["dsum23"], 1)
                    pool.wait_ge(ev["dsum23"], n["m"])
                    nc.gpsimd.tensor_tensor(DSUM[:, 2, :], DSUM[:, 0, :], DSUM[:, 1, :], ALU.add).then_inc(
                        ev["dsum_ready"], 1)
                if front:
                    pool.wait_ge(ev["a0h_23"], n["f"])
                    nc.gpsimd.tensor_tensor(A0L[:, 2:4, :], A0[:, 2:4, :], A0H[:, 2:4, :].bitcast(F32),
                                            ALU.subtract).then_inc(ev["a0l_23"], 1)
                if rear:
                    pool.wait_ge(ev["ssu_ready"], n["r"])
                    nc.gpsimd.tensor_tensor(T[:, 17, :], T[:, 16, :], POW[:, 1, :], ALU.pow).then_inc(
                        ev["nu_pow"], 1)
                if front:
                    pool.wait_ge(ev["a0h_01"], n["f"])
                    nc.gpsimd.tensor_tensor(A0L[:, 0:2, :], A0[:, 0:2, :], A0H[:, 0:2, :].bitcast(F32),
                                            ALU.subtract).then_inc(ev["a0l_01"], 1)
                if rear:
                    rstd(2, n["ln2"])
                if mid:
                    pool.wait_ge(ev["a1_01"], n["m"])
                    nc.gpsimd.tensor_tensor(ASUM[:, 0, :], A1[:, 0, :], A1[:, 1, :], ALU.add).then_inc(
                        ev["asum01"], 1)
                    pool.wait_ge(ev["d_safe"], n["m"])
                    nc.gpsimd.tensor_tensor(D[:, 3, :], D[:, 2, :], POW[:, 0, :], ALU.pow).then_inc(ev["d_pow"], 1)
                    pool.wait_ge(ev["dis_eps"], n["m"])
                    pool.wait_ge(ev["dis_kept"], n["r"])
                    nc.gpsimd.tensor_tensor(DIS[:, :], D[:, 5, :], POW[:, 0, :], ALU.pow).then_inc(
                        ev["dis_ready"], 1)
                    for half, name in ((0, "adjh_01"), (1, "adjh_23")):
                        pool.wait_ge(ev[name], n["m"])
                        h = slice(2 * half, 2 * half + 2)
                        last = nc.gpsimd.tensor_tensor(ADJL[:, h, :], ADJM[:, h, :], ADJH[:, h, :].bitcast(F32),
                                                       ALU.subtract)
                    last.then_inc(ev["adjl_ready"], 1)
                if rear:
                    rstd(3, n["ln3"])
                if front and (not isinstance(t, int) or t + 1 < B):
                    rest_of_h1(n["f_next"], n["f"])
                if mid:
                    pool.wait_ge(ev["var_ready"], n["m"])
                    nc.gpsimd.tensor_tensor(RSTD[:, 3:5, :], VEPS[:, 3:5, :], POW[:, :, :], ALU.pow).then_inc(
                        ev["ln_rstd"], 1)
                    shift(1, 3, n["ln1"])

            rest_of_h1(1, 0)
            slots(pool, body)

        @block.scalar
        def _(act):
            A = nc.scalar.activation
            act.wait_ge(s_const, 64)

            def row_squares(out, tile, name):
                for c in range(C):
                    last = A(JUNK[:, c, :], tile(c), ACT.Square, accum_out=out[:, c:c + 1])
                last.then_inc(ev[name], 1)

            def leading_x(count, previous):
                act.wait_ge(ev["x_loaded"], 16 * count)
                act.wait_ge(ev["x_used"], previous)
                A(XH[:, :], X_IN[:, :], ACT.Copy).then_inc(ev["xh"], 1)

            def norm_apply(layer, src, dst, count):
                act.wait_ge(ev["ln_shift"], count)
                row = ROW[layer]
                for c in range(C):
                    last = A(dst[:, c, :], src(c), ACT.Identity, bias=SHIFT[:, layer, c:c + 1],
                             scale=RSTD[:, row, c:c + 1])
                return last

            def first_conv(count, previous):
                act.wait_ge(ev["conv1_done"], count)
                act.wait_ge(ev["h1l_ready"], previous)
                act.wait_ge(ev["conv2_done"], previous)
                A(H1H[:, HALF:HALF + N], CONV[:, :], ACT.Relu, bias=BI[:, 0:1], scale=SC[:, 0:1])
                A(H1[:, :], CONV[:, :], ACT.Relu, bias=BI[:, 0:1], scale=SC[:, 0:1]).then_inc(ev["h1_ready"], 1)

            def squares(count):
                act.wait_ge(ev["g1_done"], count)
                A(SQ[:, :], F1[:, :], ACT.Square, bias=PAR[:, SQ_BIAS:SQ_BIAS + 1]).then_inc(ev["sq_ready"], 1)

            def parts(count):
                act.wait_ge(ev["g_done"], count)
                A(ZL[:, :], F1[:, :], ACT.Identity, bias=PAR[:, L_ZC:L_ZC + 1],
                  scale=PAR[:, L_ZA:L_ZA + 1])
                A(ZR[:, :], F1[:, :], ACT.Identity, bias=PAR[:, R_ZC:R_ZC + 1],
                  scale=PAR[:, R_ZA:R_ZA + 1]).then_inc(ev["zr_ready"], 1)

            def output(stored, count):
                act.wait_ge(ev["out_stored"], stored)
                norm_apply(3, lambda c: Z3[:, c, :], OUT, count).then_inc(ev["out_ready"], 1)

            leading_x(1, 0)
            squares(1)
            act.wait_ge(s_bn, 1)
            first_conv(1, 0)
            parts(1)

            def body(t, front, mid, rear):
                n = counts(act, t)

                def exps(a, b):
                    for c in range(a, b):
                        act.wait_ge(ev["dist_done"], nth(c, n["f"]))
                        A(A0[:, c, :], CB[c % 2][:, :], ACT.Exp).then_inc(ev["exp_ready"], 1)

                def sigmoids(a, b):
                    for c in range(a, b):
                        act.wait_ge(ev["att_done"], nth(c, n["m"]))
                        A(SIG[:, c, :], CB[c % 2][:, :], ACT.Sigmoid, scale=float(P) ** -0.5).then_inc(
                            ev["sig_ready"], 1)

                if mid:
                    act.wait_ge(ev["gate_u"], n["m"])
                    A(NG[:, :], GT[:, :], ACT.Tanh, bias=PAR[:, BI_N:BI_N + 1]).then_inc(ev["n_ready"], 1)
                nc.scalar.preload_act_table_set("natural_log_exp_and_others")
                if front:
                    exps(0, 2)
                if rear:
                    act.wait_ge(ev["z2_ready"], n["r_prev"])
                    norm_apply(1, lambda c: Z1[:, c, :], X2, n["ln1_prev"]).then_inc(ev["x2_ready"], 1)
                    act.wait_ge(ev["ratio_ready"], n["r"])
                    A(T[:, 7, :], T[:, 6, :], ACT.Ln).then_inc(ev["ln_ready"], 1)
                if front:
                    exps(2, C)
                    act.wait_ge(ev["x_loaded"], 16 * n["f"])
                    act.wait_ge(ev["y_ready"], n["m"])
                    A(XT[:, :], X_IN[:, :], ACT.Copy).then_inc(ev["xcopy"], 1)
                nc.scalar.preload_act_table_set("sigmoid_and_others")
                if mid:
                    act.wait_ge(ev["z1_ready"], n["m_prev"])
                    norm_apply(0, lambda c: cols(K0, c), X1, n["ln0"]).then_inc(ev["x1_ready"], 1)
                    act.wait_ge(ev["x1t_done"], n["m"])
                    A(X1H[:, :], K2[:, :], ACT.Copy).then_inc(ev["x1th_ready"], 1)
                if front:
                    act.wait_ge(ev["agg0_done"], n["f_prev"])
                    act.wait_ge(ev["a0_23"], n["f"])
                    A(A0H[:, 2:4, :], A0[:, 2:4, :], ACT.Copy).then_inc(ev["a0h_23"], 1)
                if rear:
                    act.wait_ge(ev["agg2_done"], n["r"])
                    act.wait_ge(ev["nat1_done"], n["m_prev"])
                    A(AG[:, :], K1[:, :], ACT.Copy).then_inc(ev["agg2_ready"], 1)
                if mid:
                    act.wait_ge(ev["k_ready"], n["m_prev"])
                    act.wait_ge(ev["q_done"], n["m"])
                    A(QRAW[:, :], K2[:, :], ACT.Copy).then_inc(ev["q_raw"], 1)
                    act.wait_ge(ev["k_done"], n["m"])
                    A(KRAW[:, :], F0[:, :], ACT.Copy).then_inc(ev["k_raw"], 1)
                if front:
                    act.wait_ge(ev["msg_added"], n["f"])
                    act.wait_ge(ev["agg0_done"], n["f_prev"])
                    A(MSH[:, :, :], MSG[:, :, :], ACT.Relu).then_inc(ev["msh_ready"], 1)
                if rear:
                    act.wait_ge(ev["nat2_done"], n["r"])
                    row_squares(T[:, 16, :], lambda c: cols(K0, c), "ssu_ready")
                if front:
                    act.wait_ge(ev["a0_01"], n["f"])
                    A(A0H[:, 0:2, :], A0[:, 0:2, :], ACT.Copy).then_inc(ev["a0h_01"], 1)
                if mid:
                    act.wait_ge(ev["a1_23"], n["m_prev"])
                    sigmoids(0, 1)
                if rear:
                    act.wait_ge(ev["nu_ready"], n["r"])
                    A(T[:, 19, :], T[:, 18, :], ACT.Tanh).then_inc(ev["tanh_ready"], 1)
                if mid:
                    sigmoids(1, C)
                if not isinstance(t, int) or t >= 3:
                    output(16 * (n["r_prev"] - 1), n["ln3_prev"])
                if rear:
                    act.wait_ge(ev["x3t_done"], n["r"])
                    A(X3T[:, :], K1[:, :], ACT.Copy).then_inc(ev["x3t_ready"], 1)
                if front:
                    act.wait_ge(ev["agg0_done"], n["f"])
                    A(NMH[:, :], F1[:, :], ACT.Copy).then_inc(ev["nmph_ready"], 1)
                if rear:
                    act.wait_ge(ev["hs_ready"], n["r"])
                    A(FH[:, :, :], HS[:, :, :], ACT.Copy).then_inc(ev["hsh_ready"], 1)
                if front:
                    act.wait_ge(ev["xconv_sum"], n["f"])
                    act.wait_ge(ev["gates_done"], n["f_prev"])
                    A(XCH[:, :], XC[:, :], ACT.Relu, bias=BI[:, 1:2])
                    A(XC[:, :], XC[:, :], ACT.Relu, bias=BI[:, 1:2]).then_inc(ev["xconv_ready"], 1)
                if rear:
                    act.wait_ge(ev["agg3_done"], n["r"])
                    act.wait_ge(ev["nat2_done"], n["r"])
                    A(AG[:, :], K1[:, :], ACT.Copy).then_inc(ev["agg3_ready"], 1)
                if front and (not isinstance(t, int) or t + 1 < B):
                    leading_x(n["f_next"], n["f"])
                if mid:
                    act.wait_ge(ev["adjm_loaded"], 16 * n["m"])
                    act.wait_ge(ev["adjl_ready"], n["m_prev"])
                    act.wait_ge(ev["agg3_done"], n["r"])
                    A(ADJH[:, 0:2, :], ADJM[:, 0:2, :], ACT.Copy).then_inc(ev["adjh_01"], 1)
                    A(ADJH[:, 2:4, :], ADJM[:, 2:4, :], ACT.Copy).then_inc(ev["adjh_23"], 1)
                    act.wait_ge(ev["agg1_done"], n["m"])
                    act.wait_ge(ev["nat3_done"], n["r"])
                    A(AG[:, :], K2[:, :], ACT.Copy).then_inc(ev["agg1_ready"], 1)
                if front:
                    act.wait_ge(ev["gater_done"], n["f"])
                    A(R[:, :], F1[:, :], ACT.Sigmoid, bias=BG[:, 0:1]).then_inc(ev["r_ready"], 1)
                if front and (not isinstance(t, int) or t + 1 < B):
                    squares(n["f_next"])
                    first_conv(n["f_next"], n["f"])
                    parts(n["f_next"])
                if front:
                    act.wait_ge(ev["gatez_done"], n["f"])
                    A(WG[:, :], C0[:, :], ACT.Sigmoid, bias=NBZ[:, :], scale=-1.0).then_inc(ev["w_ready"], 1)

            slots(act, body)
            output(16 * (B - 1), 4 * B)

        @block.vector
        def _(dve):
            V = nc.vector
            V.memset(H1H[:, :].bitcast(F32), 0.0)
            V.memset(H1L[:, :].bitcast(F32), 0.0).then_inc(s_set, 1)

            def split(first, last, count):
                V.tensor_copy(WH[:, first:last], W[:, first:last]).then_inc(s_leading, 1)
                dve.wait_ge(s_leading, count)
                V.tensor_tensor(WL[:, first:last], W[:, first:last], WH[:, first:last].bitcast(F32),
                                ALU.subtract).then_inc(s_split, 1)

            dve.wait_ge(s_first_w, 16)
            split(0, W_CONV2, 1)
            dve.wait_ge(s_const, 64)
            V.tensor_scalar(VE[:, 0:1], PAR[:, V1:V1 + 1], BN_EPS, None, ALU.add)
            V.tensor_scalar(VE[:, 1:2], PAR[:, V2:V2 + 1], BN_EPS, None, ALU.add)
            V.tensor_tensor(BG[:, 0:1], PAR[:, BI_R:BI_R + 1], PAR[:, BH_R:BH_R + 1], ALU.add)
            V.tensor_tensor(BG[:, 1:2], PAR[:, BI_Z:BI_Z + 1], PAR[:, BH_Z:BH_Z + 1], ALU.add).then_inc(s_prep, 1)
            dve.wait_ge(s_prep, 1)
            V.tensor_scalar(NBZ[:, :], BG[:, 1:2], -1.0, None, ALU.mult)
            dve.wait_ge(s_bn_pow, 1)
            V.tensor_tensor(SC[:, 0:1], PAR[:, G1:G1 + 1], RS[:, 0:1], ALU.mult)
            V.tensor_tensor(SC[:, 1:2], PAR[:, G2:G2 + 1], RS[:, 1:2], ALU.mult).then_inc(s_prep, 1)
            dve.wait_ge(s_prep, 2)
            V.tensor_tensor(MS[:, 0:1], PAR[:, M1:M1 + 1], SC[:, 0:1], ALU.mult)
            V.tensor_tensor(MS[:, 1:2], PAR[:, M2:M2 + 1], SC[:, 1:2], ALU.mult).then_inc(s_prep, 1)
            dve.wait_ge(s_prep, 3)
            V.tensor_tensor(BI[:, 0:1], PAR[:, B1:B1 + 1], MS[:, 0:1], ALU.subtract)
            V.tensor_tensor(BI[:, 1:2], PAR[:, B2:B2 + 1], MS[:, 1:2], ALU.subtract).then_inc(s_bn, 1)

            def norm_stats(layer, src, count):
                L = LT[:, layer, :, :]
                for c in range(C):
                    last = V.bn_stats(ST[:, layer, c, :], src(c))
                last.then_inc(ev["ln_stats"], 1)
                dve.wait_ge(ev["ln_stats"], count)
                even, odd = (lambda k, h=h: ST[:, layer, :, 3 * h + k] for h in (0, 1))
                V.tensor_tensor(L[:, 0, :], even(1), odd(1), ALU.add)
                V.tensor_tensor(L[:, 1, :], even(1), odd(1), ALU.subtract)
                V.tensor_tensor(L[:, 2, :], even(2), odd(2), ALU.add).then_inc(ev["ln_sums"], 1)
                dve.wait_ge(ev["ln_sums"], count)
                V.tensor_scalar(NMEAN[:, layer, :], L[:, 0, :], -0.5, None, ALU.mult)
                V.scalar_tensor_tensor(L[:, 3, :], L[:, 1, :], 0.25, L[:, 1, :], ALU.mult, ALU.mult)
                V.tensor_scalar(L[:, 4, :], L[:, 2, :], 1 / P, LN_EPS, ALU.mult, ALU.add).then_inc(
                    ev["ln_parts"], 1)
                dve.wait_ge(ev["ln_parts"], count)
                V.tensor_tensor(VEPS[:, ROW[layer], :], L[:, 3, :], L[:, 4, :], ALU.add).then_inc(ev["ln_eps"], 1)

            def norm_apply(layer, src, dst, count):
                dve.wait_ge(ev["ln_rstd"], count)
                for c in range(C):
                    last = V.tensor_scalar(dst[:, c, :], src(c), NMEAN[:, layer, c:c + 1],
                                           RSTD[:, ROW[layer], c:c + 1], ALU.add, ALU.mult)
                return last

            def rest_of_x(count, previous):
                dve.wait_ge(ev["x_loaded"], 16 * count)
                dve.wait_ge(ev["xh"], count)
                dve.wait_ge(ev["x_used"], previous)
                V.tensor_tensor(XL[:, :], X_IN[:, :], XH[:, :].bitcast(F32), ALU.subtract).then_inc(ev["xl"], 1)

            def stacked(count):
                dve.wait_ge(ev["zr_ready"], count)
                V.scalar_tensor_tensor(STL[:, :], F1[:, :], PAR[:, L_A:L_A + 1], ZL[:, :].bitcast(F32),
                                       ALU.mult, ALU.subtract)
                V.scalar_tensor_tensor(STR[:, :], F1[:, :], PAR[:, R_A:R_A + 1], ZR[:, :].bitcast(F32),
                                       ALU.mult, ALU.subtract).then_inc(ev["str_ready"], 1)

            rest_of_x(1, 0)
            dve.wait_ge(s_conv2_w, 16)
            split(W_CONV2, W_LIN, 2)
            stacked(1)
            dve.wait_ge(s_rest_w, 32)
            split(W_LIN, W_SPLIT, 3)

            def body(t, front, mid, rear):
                n = counts(dve, t)
                f, m, r = n["f"], n["m"], n["r"]

                def bias_row(k):
                    return ROWS[:, k, :].unsqueeze(1).to_broadcast([P, C, P])

                def masked0(a, b):
                    for c in range(a, b):
                        dve.wait_ge(ev["exp_ready"], nth(c, f))
                        last = V.tensor_tensor(A0[:, c, :], A0[:, c, :], ADJF[:, c, :], ALU.mult)
                    return last

                def masked1(a, b):
                    for c in range(a, b):
                        dve.wait_ge(ev["sig_ready"], nth(c, m))
                        last = V.tensor_tensor(A1[:, c, :], SIG[:, c, :], ADJM[:, c, :], ALU.mult)
                    return last

                if rear:
                    dve.wait_ge(ev["ln_rstd"], n["ln1_prev"])
                    V.scalar_tensor_tensor(T[:, 1, :], RSTD[:, 4, :], P ** 0.5, RSTD[:, 3, :], ALU.mult,
                                           ALU.mult).then_inc(ev["nrm_ready"], 1)
                if mid:
                    dve.wait_ge(ev["n_ready"], m)
                    V.tensor_tensor(NG[:, :], NG[:, :], XT[:, :], ALU.subtract).then_inc(ev["gate_d"], 1)
                    dve.wait_ge(ev["gate_d"], m)
                    dve.wait_ge(ev["w_ready"], m)
                    V.tensor_tensor(NG[:, :], NG[:, :], WG[:, :], ALU.mult).then_inc(ev["gate_e"], 1)
                    dve.wait_ge(ev["gate_e"], m)
                    V.scalar_tensor_tensor(Y[:, :], XT[:, :], 2.0, NG[:, :], ALU.mult, ALU.add).then_inc(
                        ev["y_ready"], 1)
                if rear:
                    dve.wait_ge(ev["nrm_ready"], r)
                    V.tensor_scalar(T[:, 2, :], T[:, 1, :], MIN_NORM, None, ALU.max)
                    V.tensor_scalar(T[:, 3, :], T[:, 1, :], MIN_NORM, ATANH_MAX, ALU.max, ALU.min).then_inc(
                        ev["z_ready"], 1)
                    dve.wait_ge(ev["z_ready"], r)
                    V.tensor_scalar(T[:, 4, :], T[:, 3, :], -1.0, 1.0, ALU.mult, ALU.add).then_inc(ev["oneminus"], 1)
                    dve.wait_ge(ev["oneminus"], r)
                    V.reciprocal(T[:, 5, :], T[:, 4, :]).then_inc(ev["rec_ready"], 1)
                    dve.wait_ge(ev["rec_ready"], r)
                    V.scalar_tensor_tensor(T[:, 6, :], T[:, 3, :], 1.0, T[:, 5, :], ALU.add, ALU.mult).then_inc(
                        ev["ratio_ready"], 1)
                if mid:
                    dve.wait_ge(ev["yt_done"], m)
                    norm_stats(0, lambda c: cols(K0, c), n["ln0"])
                if rear:
                    V.reciprocal(T[:, 8, :], T[:, 2, :])
                    V.tensor_scalar(T[:, 14, :], T[:, 3, :], SERIES_BELOW, None, ALU.is_lt)
                    V.tensor_tensor(T[:, 9, :], T[:, 3, :], T[:, 3, :], ALU.mult).then_inc(ev["w_sq"], 1)
                    dve.wait_ge(ev["w_sq"], r)
                    V.scalar_tensor_tensor(T[:, 10, :], T[:, 9, :], 7 / 5, T[:, 9, :], ALU.add, ALU.mult).then_inc(
                        ev["ser1"], 1)
                    dve.wait_ge(ev["ser1"], r)
                    V.scalar_tensor_tensor(T[:, 11, :], T[:, 10, :], 7 / 3, T[:, 9, :], ALU.add, ALU.mult).then_inc(
                        ev["ser2"], 1)
                    dve.wait_ge(ev["ser2"], r)
                    V.tensor_scalar(T[:, 13, :], T[:, 11, :], 1 / 7, 1.0, ALU.mult, ALU.add).then_inc(ev["ser3"], 1)
                    dve.wait_ge(ev["ser3"], r)
                    dve.wait_ge(ev["ln_ready"], r)
                    V.scalar_tensor_tensor(T[:, 22, :], T[:, 7, :], 0.5, T[:, 8, :], ALU.mult, ALU.mult).then_inc(
                        ev["main_f"], 1)
                    dve.wait_ge(ev["main_f"], r)
                    V.tensor_tensor(T[:, 23, :], T[:, 13, :], T[:, 22, :], ALU.subtract).then_inc(ev["diff_f"], 1)
                    dve.wait_ge(ev["diff_f"], r)
                    V.tensor_tensor(T[:, 24, :], T[:, 23, :], T[:, 14, :], ALU.mult).then_inc(ev["mix_f"], 1)
                    dve.wait_ge(ev["mix_f"], r)
                    V.tensor_tensor(T[:, 25, :], T[:, 22, :], T[:, 24, :], ALU.add).then_inc(ev["f_ready"], 1)
                    dve.wait_ge(ev["f_ready"], r)
                    dve.wait_ge(ev["x2_ready"], r)
                    dve.wait_ge(ev["agg3_done"], n["r_prev"])
                    V.tensor_tensor(FH[:, :, :], X2[:, :, :], spread(T[:, 25, :]), ALU.mult).then_inc(
                        ev["xth_ready"], 1)
                    dve.wait_ge(ev["xth_ready"], r)
                    for c in range(C):
                        last = V.scalar_tensor_tensor(FL[:, c, :], X2[:, c, :], T[:, 25, c:c + 1],
                                                      FH[:, c, :].bitcast(F32), ALU.mult, ALU.subtract)
                    last.then_inc(ev["xt_ready"], 1)
                if mid:
                    dve.wait_ge(ev["x1th_ready"], m)
                    V.tensor_tensor(X1L[:, :], K2[:, :], X1H[:, :].bitcast(F32), ALU.subtract).then_inc(
                        ev["x1tl_ready"], 1)
                if front:
                    dve.wait_ge(ev["adjf_loaded"], 16 * f)
                    dve.wait_ge(ev["agg0_done"], n["f_prev"])
                    masked0(0, C // 2).then_inc(ev["a0_01"], 1)
                    dve.wait_ge(ev["msg_done"], f)
                    dve.wait_ge(ev["msl_ready"], n["f_prev"])
                    V.tensor_tensor(MSG[:, :, :], chunked(F0), bias_row(0), ALU.add).then_inc(ev["msg_added"], 1)
                if mid:
                    dve.wait_ge(ev["q_raw"], m)
                    dve.wait_ge(ev["att_done"], nth(C - 1, n["m_prev"]))
                    V.scalar_tensor_tensor(QT[:, :], QRAW[:, :], SLOPE, QRAW[:, :], ALU.mult, ALU.max).then_inc(
                        ev["q_ready"], 1)
                    dve.wait_ge(ev["k_raw"], m)
                    V.scalar_tensor_tensor(KT[:, :], KRAW[:, :], SLOPE, KRAW[:, :], ALU.mult, ALU.max).then_inc(
                        ev["k_ready"], 1)
                if front:
                    dve.wait_ge(ev["msh_ready"], f)
                    V.scalar_tensor_tensor(MSL[:, :, :], MSG[:, :, :], 0.0, MSH[:, :, :].bitcast(F32), ALU.max,
                                           ALU.subtract).then_inc(ev["msl_ready"], 1)
                if mid:
                    dve.wait_ge(ev["x_done"], m)
                    V.tensor_tensor(XX[:, :, :], chunked(K1), bias_row(1), ALU.add).then_inc(ev["x_added"], 1)
                    dve.wait_ge(ev["x_added"], m)
                    V.scalar_tensor_tensor(XX[:, :, :], XX[:, :, :], SLOPE, XX[:, :, :], ALU.mult,
                                           ALU.max).then_inc(ev["xact_ready"], 1)
                if rear:
                    dve.wait_ge(ev["nu_pow"], r)
                    V.tensor_scalar(T[:, 18, :], T[:, 17, :], MIN_NORM, None, ALU.max).then_inc(ev["nu_ready"], 1)
                    dve.wait_ge(ev["nu_ready"], r)
                    V.reciprocal(T[:, 20, :], T[:, 18, :]).then_inc(ev["rnu_ready"], 1)
                    dve.wait_ge(ev["rnu_ready"], r)
                    dve.wait_ge(ev["tanh_ready"], r)
                    V.tensor_tensor(T[:, 21, :], T[:, 19, :], T[:, 20, :], ALU.mult).then_inc(ev["g_ready"], 1)
                    dve.wait_ge(ev["g_ready"], r)
                    V.tensor_tensor(T[:, 26, :], T[:, 21, :], T[:, 17, :], ALU.mult).then_inc(ev["ny_ready"], 1)
                    dve.wait_ge(ev["ny_ready"], r)
                    V.tensor_scalar(T[:, 27, :], T[:, 26, :], MIN_NORM, None, ALU.max).then_inc(ev["nyc_ready"], 1)
                    dve.wait_ge(ev["nyc_ready"], r)
                    V.reciprocal(T[:, 28, :], T[:, 27, :]).then_inc(ev["rny_ready"], 1)
                    dve.wait_ge(ev["rny_ready"], r)
                    V.tensor_scalar(T[:, 29, :], T[:, 28, :], BALL, 1.0, ALU.mult, ALU.min).then_inc(
                        ev["fac_ready"], 1)
                    dve.wait_ge(ev["fac_ready"], r)
                    V.tensor_tensor(T[:, 30, :], T[:, 21, :], T[:, 29, :], ALU.mult).then_inc(ev["g2_ready"], 1)
                    dve.wait_ge(ev["g2_ready"], r)
                    for c in range(C):
                        last = V.scalar_tensor_tensor(Z2[:, c, :], cols(K0, c), T[:, 30, c:c + 1], X2[:, c, :],
                                                      ALU.mult, ALU.add)
                    last.then_inc(ev["z2_ready"], 1)
                    dve.wait_ge(ev["z2_ready"], r)
                    norm_stats(2, lambda c: Z2[:, c, :], n["ln2"])
                if mid:
                    dve.wait_ge(ev["adjm_loaded"], 16 * m)
                    dve.wait_ge(ev["agg1_done"], n["m_prev"])
                    masked1(0, 2).then_inc(ev["a1_01"], 1)
                if rear:
                    norm_apply(2, lambda c: Z2[:, c, :], X3, n["ln2"]).then_inc(ev["x3_ready"], 1)
                if mid:
                    masked1(2, C).then_inc(ev["a1_23"], 1)
                    dve.wait_ge(ev["a1_23"], m)
                    dve.wait_ge(ev["deg_done"], n["m_prev"])
                    V.tensor_tensor(ASUM[:, 1, :], A1[:, 2, :], A1[:, 3, :], ALU.add).then_inc(ev["asum23"], 1)
                    dve.wait_ge(ev["asum23"], m)
                    dve.wait_ge(ev["asum01"], m)
                    V.tensor_tensor(ASUM[:, 2, :], ASUM[:, 0, :], ASUM[:, 1, :], ALU.add).then_inc(
                        ev["asum_ready"], 1)
                if rear:
                    dve.wait_ge(ev["dis_ready"], r)
                    dve.wait_ge(ev["res_scaled"], n["r_prev"])
                    V.tensor_copy(DIS_R[:, :], DIS[:, :]).then_inc(ev["dis_kept"], 1)
                    dve.wait_ge(ev["hlin_done"], r)
                    V.tensor_tensor(HS[:, :, :], chunked(K2), bias_row(2), ALU.add).then_inc(ev["hlin_added"], 1)
                    dve.wait_ge(ev["dis_kept"], r)
                    dve.wait_ge(ev["hlin_added"], r)
                    V.tensor_tensor(HS[:, :, :], HS[:, :, :], spread(DIS_R[:, :]), ALU.mult).then_inc(
                        ev["hs_ready"], 1)
                if front:
                    dve.wait_ge(ev["nmph_ready"], f)
                    V.tensor_tensor(NML[:, :], F1[:, :], NMH[:, :].bitcast(F32), ALU.subtract).then_inc(
                        ev["nmpl_ready"], 1)
                if rear:
                    dve.wait_ge(ev["mask_loaded"], 16 * r)
                    V.tensor_tensor(DM[:, :], DIS_R[:, :], MASK[:, :], ALU.mult).then_inc(ev["dm_ready"], 1)
                    dve.wait_ge(ev["hsh_ready"], r)
                    V.tensor_tensor(FL[:, :, :], HS[:, :, :], FH[:, :, :].bitcast(F32), ALU.subtract).then_inc(
                        ev["hsl_ready"], 1)
                if mid:
                    dve.wait_ge(ev["deg_done"], m)
                    V.tensor_copy(D[:, 0, :], K0[:, 0:C])
                    V.tensor_scalar(D[:, 5, :], K0[:, C:2 * C], 1.0, DEG_EPS, ALU.add, ALU.add).then_inc(
                        ev["dis_eps"], 1)
                    dve.wait_ge(ev["dis_eps"], m)
                    V.tensor_scalar(D[:, 1, :], D[:, 0, :], 0.0, None, ALU.is_equal).then_inc(ev["d_zero"], 1)
                    dve.wait_ge(ev["d_zero"], m)
                    V.tensor_tensor(D[:, 2, :], D[:, 0, :], D[:, 1, :], ALU.add).then_inc(ev["d_safe"], 1)
                    dve.wait_ge(ev["d_safe"], m)
                    V.tensor_scalar(D[:, 4, :], D[:, 1, :], -1.0, 1.0, ALU.mult, ALU.add).then_inc(ev["d_mask"], 1)
                    dve.wait_ge(ev["d_mask"], m)
                if front:
                    dve.wait_ge(ev["conv2_done"], f)
                    dve.wait_ge(ev["xcopy"], f)
                    V.scalar_tensor_tensor(XC[:, :], CONV[:, :], SC[:, 1:2], XT[:, :], ALU.mult, ALU.add).then_inc(
                        ev["xconv_sum"], 1)
                if mid:
                    dve.wait_ge(ev["d_pow"], m)
                    V.tensor_tensor(DINV[:, :], D[:, 3, :], D[:, 4, :], ALU.mult).then_inc(ev["dinv_ready"], 1)
                    dve.wait_ge(ev["dinv_ready"], m)
                    dve.wait_ge(ev["xact_ready"], m)
                    V.tensor_tensor(XS[:, :, :], XX[:, :, :], spread(DINV[:, :]), ALU.mult).then_inc(
                        ev["xs_ready"], 1)
                if front:
                    dve.wait_ge(ev["xconv_ready"], f)
                    V.tensor_tensor(XCL[:, :], XC[:, :], XCH[:, :].bitcast(F32), ALU.subtract).then_inc(
                        ev["xcl_ready"], 1)
                if rear:
                    dve.wait_ge(ev["nat3_done"], r)
                    V.tensor_tensor(RES[:, :, :], chunked(K0), HS[:, :, :], ALU.add).then_inc(ev["res_ready"], 1)
                if front and (not isinstance(t, int) or t + 1 < B):
                    rest_of_x(n["f_next"], f)
                if rear:
                    dve.wait_ge(ev["res_ready"], r)
                    dve.wait_ge(ev["dm_ready"], r)
                    dve.wait_ge(ev["out_ready"], n["r_prev"])
                    V.tensor_tensor(RES[:, :, :], RES[:, :, :], spread(DM[:, :]), ALU.mult).then_inc(
                        ev["res_scaled"], 1)
                    dve.wait_ge(ev["res_scaled"], r)
                    V.scalar_tensor_tensor(Z3[:, :, :], RES[:, :, :], 0.0, X3[:, :, :], ALU.max, ALU.add).then_inc(
                        ev["z3_ready"], 1)
                    dve.wait_ge(ev["z3_ready"], r)
                    norm_stats(3, lambda c: Z3[:, c, :], n["ln3"])
                if front:
                    dve.wait_ge(ev["r_ready"], f)
                    V.scalar_tensor_tensor(GT[:, :], F0[:, :], PAR[:, BH_N:BH_N + 1], R[:, :], ALU.add,
                                           ALU.mult).then_inc(ev["gate_t"], 1)
                    dve.wait_ge(ev["gate_t"], f)
                if mid:
                    dve.wait_ge(ev["nat1_done"], m)
                    dve.wait_ge(ev["x2_ready"], n["m_prev"])
                    for c in range(C):
                        last = V.scalar_tensor_tensor(Z1[:, c, :], cols(K1, c), DINV[:, c:c + 1], X1[:, c, :],
                                                      ALU.mult, ALU.add)
                    last.then_inc(ev["z1_ready"], 1)
                    dve.wait_ge(ev["z1_ready"], m)
                    norm_stats(1, lambda c: Z1[:, c, :], n["ln1"])
                    V.scalar_tensor_tensor(VEPS[:, 4, :], LT[:, 1, 2, :], 1 / P, LT[:, 1, 3, :], ALU.mult,
                                           ALU.add).then_inc(ev["var_ready"], 1)
                if front:
                    dve.wait_ge(ev["gates_done"], f)
                    V.tensor_tensor(GT[:, :], GT[:, :], C1[:, :], ALU.add).then_inc(ev["gate_u"], 1)
                if front and (not isinstance(t, int) or t + 1 < B):
                    stacked(n["f_next"])

            slots(dve, body)

        @block.tensor
        def _(pe):
            mm = nc.tensor.matmul

            def product(out, terms):
                k = 0
                for wgt, mov in terms:
                    for i, j in ((0, 0), (0, 1), (1, 0)):
                        last = mm(out, wgt[i], mov[j], start=(k == 0), stop=(k == 3 * len(terms) - 1))
                        k += 1
                return last

            def weight(at_col):
                return WH[:, at_col:at_col + P], WL[:, at_col:at_col + P]

            def transposed(out, tile):
                for c in range(C):
                    last = nc.tensor.transpose(cols(out, c), tile(c), IDENT[:, :])
                return last

            def aggregate_whole(out, rows, chunks):
                for c in range(C):
                    last = mm(out[:, :], rows[:, c, :], chunks[:, c, :], start=(c == 0), stop=(c == C - 1))
                return last

            def aggregate(out, rows, chunks):
                for c in range(C):
                    for i, (a, b) in enumerate(((0, 0), (0, 1), (1, 0))):
                        last = mm(out[:, :], rows[a][:, c, :], chunks[b][:, c, :], start=(c == 0 and i == 0),
                                  stop=(c == C - 1 and i == 2))
                return last

            pe.wait_ge(s_const, 64)
            pe.wait_ge(s_split, 1)
            pe.wait_ge(s_set, 4)

            def first_conv(count, previous):
                pe.wait_ge(ev["xl"], count)
                pe.wait_ge(ev["xconv_sum"], previous)
                product(CONV[:, :], [(weight(W_CONV1), (XH[:, :], XL[:, :]))]).then_inc(ev["conv1_done"], 1)

            def factors(previous):
                pe.wait_ge(ev["r_ready"], previous)
                product(F1[:, :], [(weight(W_SE), (XH[:, :], XL[:, :]))]).then_inc(ev["g1_done"], 1)

            def own_squares(count):
                pe.wait_ge(ev["sq_ready"], count)
                mm(F1[:, :], SQMAT[:, :], SQ[:, :], start=False, stop=True, skip_group_check=True).then_inc(
                    ev["g_done"], 1)

            first_conv(1, 0)
            factors(0)
            own_squares(1)

            def body(t, front, mid, rear):
                n = counts(pe, t)
                f, m, r = n["f"], n["m"], n["r"]
                xt = (XH[:, :], XL[:, :])
                x1t = (X1H[:, :], X1L[:, :])

                def taps(a, b):
                    for k in range(a, b):
                        for i, (w, h) in enumerate(((WH, H1H), (WH, H1L), (WL, H1H))):
                            last = mm(CONV[:, :], w[:, W_CONV2 + k * P:W_CONV2 + (k + 1) * P], h[:, k:k + N],
                                      start=(k == 0 and i == 0), stop=(k == TAPS - 1 and i == 2))
                    return last

                xc, nm = (XCH[:, :], XCL[:, :]), (NMH[:, :], NML[:, :])

                def gate(bank, first, last, terms):
                    k = 0
                    for wgt, mov in terms:
                        for i, j in ((0, 0), (0, 1), (1, 0)):
                            k += 1
                            done = mm(bank[:, :], wgt[i], mov[j], start=(first and k == 1),
                                      stop=(last and k == 3 * len(terms)))
                    return done

                def messages():
                    for c in range(C):
                        last = product(cols(F0, c), [((cols(XH, c), cols(XL, c)), weight(W_MSG))])
                    return last

                def distances(c):
                    mm(CB[c % 2][:, :], cols(STL, c), STR[:, :], start=True, stop=True).then_inc(
                        ev["dist_done"], 1)

                if front:
                    pe.wait_ge(ev["gate_t"], n["f_prev"])
                    messages().then_inc(ev["msg_done"], 1)
                    pe.wait_ge(ev["h1_ready"], f)
                    pe.wait_ge(ev["h1l_ready"], f)
                    if isinstance(t, int) and t == 0:
                        pe.wait_ge(s_split, 2)
                    taps(0, 2)
                    pe.wait_ge(ev["str_ready"], f)
                    pe.wait_ge(ev["w_ready"], n["f_prev"])
                    distances(0)
                    pe.wait_ge(ev["gate_u"], n["f_prev"])
                    distances(1)
                    taps(2, 4)
                if mid:
                    pe.wait_ge(ev["y_ready"], m)
                    pe.wait_ge(ev["res_ready"], n["r_prev"])
                    transposed(K0, lambda c: cols(Y, c)).then_inc(ev["yt_done"], 1)
                if front:
                    pe.wait_ge(ev["exp_ready"], nth(0, f))
                    distances(2)
                    pe.wait_ge(ev["exp_ready"], nth(1, f))
                    distances(3)
                    taps(4, 11)
                if mid:
                    pe.wait_ge(ev["x1_ready"], m)
                    pe.wait_ge(ev["agg1_ready"], n["m_prev"])
                    transposed(K2, lambda c: X1[:, c, :]).then_inc(ev["x1t_done"], 1)
                if rear:
                    pe.wait_ge(ev["xt_ready"], r)
                    pe.wait_ge(ev["adjl_ready"], r)
                    pe.wait_ge(ev["z1_ready"], n["m_prev"])
                    aggregate(K1, (FH, FL), (ADJH, ADJL)).then_inc(ev["agg2_done"], 1)
                if mid:
                    pe.wait_ge(ev["x1tl_ready"], m)
                    pe.wait_ge(ev["x1th_ready"], m)
                    product(K2[:, :], [(weight(W_Q), x1t)]).then_inc(ev["q_done"], 1)
                    pe.wait_ge(ev["msg_added"], f)
                    product(F0[:, :], [(weight(W_K), x1t)]).then_inc(ev["k_done"], 1)
                if rear:
                    pe.wait_ge(ev["agg2_ready"], r)
                    pe.wait_ge(ev["x1_ready"], m)
                    transposed(K0, lambda c: cols(AG, c)).then_inc(ev["nat2_done"], 1)
                if mid:
                    pe.wait_ge(ev["agg2_ready"], r)
                    for c in range(C):
                        last = product(cols(K1, c), [((cols(X1H, c), cols(X1L, c)), weight(W_LIN))])
                    last.then_inc(ev["x_done"], 1)
                if front:
                    taps(11, 12)
                if mid:
                    pe.wait_ge(ev["q_ready"], m)
                    pe.wait_ge(ev["k_ready"], m)
                    for c in range(C):
                        if c < 2:
                            pe.wait_ge(ev["exp_ready"], nth(c + 2, f))
                        else:
                            pe.wait_ge(ev["sig_ready"], nth(c - 2, m))
                        mm(CB[c % 2][:, :], cols(KT, c), QT[:, :], start=True, stop=True).then_inc(
                            ev["att_done"], 1)
                if front:
                    pe.wait_ge(ev["msl_ready"], f)
                    pe.wait_ge(ev["a0l_01"], f)
                    pe.wait_ge(ev["a0l_23"], f)
                    aggregate(F1, (MSH, MSL), (A0H, A0L)).then_inc(ev["agg0_done"], 1)
                    taps(12, 14)
                    if isinstance(t, int) and t == 0:
                        pe.wait_ge(s_split, 3)
                        pe.wait_ge(s_rest_w, 32)
                    pe.wait_ge(ev["sig_ready"], nth(2, m))
                    gate(C0, True, False, [(weight(W_HH + P), xt)])
                    pe.wait_ge(ev["k_raw"], m)
                    gate(F0, True, True, [(weight(W_HH + 2 * P), xt)])
                if rear:
                    pe.wait_ge(ev["x3_ready"], r)
                    pe.wait_ge(ev["x_added"], m)
                    transposed(K1, lambda c: X3[:, c, :]).then_inc(ev["x3t_done"], 1)
                if front:
                    taps(14, 16)
                if rear:
                    pe.wait_ge(ev["x3t_ready"], r)
                    pe.wait_ge(ev["q_raw"], m)
                    for c in range(C):
                        last = mm(cols(K2, c), cols(X3T, c), WOUT[:, :], start=True, stop=True)
                    last.then_inc(ev["hlin_done"], 1)
                if mid:
                    pe.wait_ge(ev["asum_ready"], m)
                    pe.wait_ge(ev["dsum_ready"], m)
                    pe.wait_ge(ev["z2_ready"], r)
                    for c in range(C):
                        mm(K0[:, c:c + 1], cols(ASUM[:, 2, :], c), ONES[:, :], start=True, stop=True)
                    for c in range(C):
                        last = mm(K0[:, C + c:C + c + 1], cols(DSUM[:, 2, :], c), ONES[:, :], start=True, stop=True)
                    last.then_inc(ev["deg_done"], 1)
                if front:
                    taps(16, TAPS).then_inc(ev["conv2_done"], 1)
                    pe.wait_ge(ev["nmpl_ready"], f)
                    pe.wait_ge(ev["nmph_ready"], f)
                    gate(F1, True, False, [(weight(W_HH), xt)]).then_inc(ev["x_used"], 1)
                if rear:
                    pe.wait_ge(ev["hsl_ready"], r)
                    aggregate(K1, (FH, FL), (ADJH, ADJL)).then_inc(ev["agg3_done"], 1)
                if front:
                    pe.wait_ge(ev["sig_ready"], nth(3, m))
                    gate(C1, True, False, [(weight(W_IH + 5 * P), nm)])
                    gate(F1, False, False, [(weight(W_IH + 3 * P), nm)])
                if rear:
                    pe.wait_ge(ev["agg3_ready"], r)
                    pe.wait_ge(ev["dis_eps"], m)
                    transposed(K0, lambda c: cols(AG, c)).then_inc(ev["nat3_done"], 1)
                if mid:
                    pe.wait_ge(ev["xs_ready"], m)
                    pe.wait_ge(ev["hlin_added"], r)
                    aggregate_whole(K2, XS, A1).then_inc(ev["agg1_done"], 1)
                if front:
                    pe.wait_ge(ev["xcl_ready"], f)
                    gate(F1, False, True, [(weight(W_IH), xc)]).then_inc(
                        ev["gater_done"], 1)
                if mid:
                    pe.wait_ge(ev["agg1_ready"], m)
                    pe.wait_ge(ev["agg3_ready"], r)
                    transposed(K1, lambda c: cols(AG, c)).then_inc(ev["nat1_done"], 1)
                if front and (not isinstance(t, int) or t + 1 < B):
                    first_conv(n["f_next"], f)
                    factors(f)
                if front:
                    gate(C0, False, True, [(weight(W_IH + 4 * P), nm), (weight(W_IH + P), xc)]).then_inc(
                        ev["gatez_done"], 1)
                if front and (not isinstance(t, int) or t + 1 < B):
                    own_squares(n["f_next"])
                if front:
                    gate(C1, False, True, [(weight(W_IH + 2 * P), xc)]).then_inc(
                        ev["gates_done"], 1)

            slots(pe, body)


def packed(i):
    t = lambda a: np.asarray(a).T
    zeros = np.zeros
    w_se = zeros((P, P), np.float32)
    for g in range(3):
        w_se[:, 5 * g:5 * g + 3] = t(i["L0_gnn_w_se"])
    conv2 = np.asarray(i["L0_gnn_conv2_w"]).transpose(1, 2, 0).reshape(P, TAPS * P)
    w_ih = np.asarray(i["L0_gnn_w_ih"])
    weights = np.concatenate(
        [t(i["L0_gnn_conv1_w"][:, :, 0]), w_se, t(i["L0_gnn_w_msg"]), conv2, i["L1_gnn_W_lin"], i["L1_gnn_W_q"],
         i["L1_gnn_W_k"], t(w_ih[:, :P]), t(w_ih[:, P:]), t(i["L0_gnn_w_hh"]), t(i["L3_gnn_W"])], axis=1)
    rows = np.broadcast_to(np.stack([i["L0_gnn_b_msg"], i["L1_gnn_b_lin"], i["L3_gnn_b"]]), (P, 3, P))
    par = zeros((P, N_PAR), np.float32)
    for k, name in enumerate(("bn1_g", "bn1_b", "bn1_m", "bn1_v", "bn2_g", "bn2_b", "bn2_m", "bn2_v")):
        par[:, k] = i["L0_gnn_" + name]
    for k, name in ((BI_R, "b_ih"), (BH_R, "b_hh")):
        par[:, k:k + 3] = t(np.asarray(i["L0_gnn_" + name]).reshape(3, P))
    sqmat = zeros((P, P), np.float32)
    par[0:3, SQ_BIAS] = i["L0_gnn_b_se"]
    par[3, SQ_BIAS] = 1
    left, right = (1, 1, 1, 0, 1), (2, 2, 2, 1, 0)
    for g in range(3):
        s = slice(5 * g, 5 * g + 5)
        par[s, L_A], par[s, R_A] = left, right
        for rest, a, za, zc, one in ((g == 1, left, L_ZA, L_ZC, 3), (g == 2, right, R_ZA, R_ZC, 4)):
            if rest:
                par[s, za] = a
            else:
                par[5 * g + one, zc] = -1
        sqmat[3, 5 * g:5 * g + 3] = i["L0_gnn_b_se"]
        sqmat[0:3, 5 * g + 3:5 * g + 5] = -1
    c = np.ascontiguousarray
    return {
        "xT": c(np.asarray(i["x"]).transpose(0, 2, 1)), "adjT": c(np.asarray(i["adj"]).transpose(0, 2, 1)),
        "mask": c(np.asarray(i["nodemask"]).reshape(B, C, P).transpose(0, 2, 1)), "weights": c(weights),
        "rows": c(rows), "params": par, "sqmat": sqmat, "ident": np.eye(P, dtype=np.float32),
    }


def kernel(**inputs):
    import concourse.bacc as bacc
    from concourse.bass_utils import run_bass_kernel_spmd

    arrays = packed(inputs)
    nc = bacc.Bacc("TRN2", target_bir_lowering=False, num_devices=1)
    args = [nc.dram_tensor("in_" + k, a.shape, mybir.dt.from_np(a.dtype), kind="ExternalInput").ap()
            for k, a in arrays.items()]
    out = nc.dram_tensor("out", (B, N, P), F32, kind="ExternalOutput").ap()
    adj_resnorm_kernel(nc, *args, out)
    got = run_bass_kernel_spmd(nc, [{"in_" + k: a for k, a in arrays.items()}], core_ids=[0])
    return got.results[0]["out"]
```
